# Optimizing a Trainium2 kernel written in Bass

```python
import numpy as np
import jax
import jax.numpy as jnp

def _softmax(x, axis=-1):
    return jax.nn.softmax(x, axis=axis)
def _gelu(x):
    return jax.nn.gelu(x, approximate=True)
def _silu(x):
    return jax.nn.silu(x)
def _sigmoid(x):
    return jax.nn.sigmoid(x)
def _layernorm(x, axis=-1, eps=1e-5):
    m = jnp.mean(x, axis=axis, keepdims=True)
    v = jnp.var(x, axis=axis, keepdims=True)
    return (x - m) / jnp.sqrt(v + eps)
def _scatter_add(tgt, idx, src, axis=0):
    return tgt.at[idx].add(src)
def _segment_sum(src, seg, n):
    return jax.ops.segment_sum(src, seg, n)

kernel_name = 'mk_conv_preact_d2_conv_nchw128_c6f1c3'

def setup_inputs(seed: int = 0):
    np.random.seed(seed)
    _w = jnp.asarray
    def _rec_inputs():
        import jax
        import jax.numpy as jnp
        _gk = jax.random.key(seed)
        x = -0.0005212 + 1 * jax.random.normal(jax.random.fold_in(_gk, 1), (104, 128, 16, 16), jnp.float32)
        return x
    x = _rec_inputs()
    def _L0_conv_setup():
        import jax, jax.numpy as jnp
        import numpy as np
        import math
        C = 128
        N_HEAD = 4
        T = 26

        def _neighbors():
            angles = [(0, 90), (0, -90)]
            for i in range(1, 4):
                angles += [(0 + 45 * j, -90 + 45 * i) for j in range(8)]
            angles = np.array(angles)
            d = np.abs(angles.reshape(26, 1, 2) - angles.reshape(1, 26, 2))
            d = np.sum(np.minimum(d, 360 - d), axis=2)
            ab = d == 45
            ab[0, -8::2] = True
            ab[-8::2, 0] = True
            ab[1, 2:10:2] = True
            ab[2:10:2, 1] = True
            sel = [np.argwhere(ab[i]).reshape(-1) for i in range(26)]
            K = max((len(s) for s in sel))
            idx = np.zeros((26, K), np.int32)
            msk = np.zeros((26, K), bool)
            for i, s in enumerate(sel):
                idx[i, :len(s)] = s
                msk[i, :len(s)] = True
            return (jnp.asarray(idx), jnp.asarray(msk))
        key = jax.random.key(seed)
        ks = jax.random.split(key, 5)
        B_total = 4 * T
        x = jax.random.normal(ks[0], (B_total, C, 16, 16), dtype=jnp.float32)
        s = 1.0 / math.sqrt(C)
        w_in = jax.random.uniform(ks[1], (3 * C, C), minval=-s, maxval=s, dtype=jnp.float32)
        b_in = jnp.zeros((3 * C,), jnp.float32)
        w_out = jax.random.uniform(ks[2], (C, C), minval=-s, maxval=s, dtype=jnp.float32)
        b_out = jnp.zeros((C,), jnp.float32)
        return {'x': x, 'w_in': w_in, 'b_in': b_in, 'w_out': w_out, 'b_out': b_out}
    _L0_conv_all = _L0_conv_setup()
    _L0_conv_in = {k: v for k, v in _L0_conv_all.items() if k in ('w_in', 'b_in', 'w_out', 'b_out', )}
    del _L0_conv_all

    def _L1_conv_setup():
        import jax, jax.numpy as jnp
        import numpy as np
        K = 9
        PAD = K // 2

        def _conv1d(x, w):
            return jax.lax.conv_general_dilated(x, w, window_strides=(1,), padding=((PAD, PAD),), dimension_numbers=('NCH', 'OIH', 'NCH'))

        def _propagate(x, w, axis, reverse):
            xm = jnp.moveaxis(x, axis, 0)
            if reverse:
                xm = xm[::-1]

            def step(prev, cur):
                new = cur + jax.nn.relu(_conv1d(prev, w))
                return (new, new)
            _, outs = jax.lax.scan(step, xm[0], xm[1:])
            res = jnp.concatenate([xm[:1], outs], axis=0)
            if reverse:
                res = res[::-1]
            return jnp.moveaxis(res, 0, axis)
        key = jax.random.key(seed)
        ks = jax.random.split(key, 5)
        B, C, H, W = (16, 128, 72, 200)
        scale = 1.0 / np.sqrt(C * K)
        x = jax.random.normal(ks[0], (B, C, H, W), dtype=jnp.float32)
        w_down = jax.random.normal(ks[1], (C, C, K), dtype=jnp.float32) * scale
        w_up = jax.random.normal(ks[2], (C, C, K), dtype=jnp.float32) * scale
        w_right = jax.random.normal(ks[3], (C, C, K), dtype=jnp.float32) * scale
        w_left = jax.random.normal(ks[4], (C, C, K), dtype=jnp.float32) * scale
        return {'x': x, 'w_down': w_down, 'w_up': w_up, 'w_right': w_right, 'w_left': w_left}
    _L1_conv_all = _L1_conv_setup()
    _L1_conv_in = {k: v for k, v in _L1_conv_all.items() if k in ('w_down', 'w_up', 'w_right', 'w_left', )}
    del _L1_conv_all

    return {
        "x": x,
        "L0_conv_w_in": _L0_conv_in["w_in"],
        "L0_conv_b_in": _L0_conv_in["b_in"],
        "L0_conv_w_out": _L0_conv_in["w_out"],
        "L0_conv_b_out": _L0_conv_in["b_out"],
        "L1_conv_w_down": _L1_conv_in["w_down"],
        "L1_conv_w_up": _L1_conv_in["w_up"],
        "L1_conv_w_right": _L1_conv_in["w_right"],
        "L1_conv_w_left": _L1_conv_in["w_left"],
    }

def reference(x, L0_conv_w_in, L0_conv_b_in, L0_conv_w_out, L0_conv_b_out, L1_conv_w_down, L1_conv_w_up, L1_conv_w_right, L1_conv_w_left):
    import jax
    import jax.numpy as jnp
    def _L0_conv_ref(x, w_in, b_in, w_out, b_out):
        import jax, jax.numpy as jnp
        import numpy as np
        import math
        C = 128
        N_HEAD = 4
        T = 26

        def _neighbors():
            angles = [(0, 90), (0, -90)]
            for i in range(1, 4):
                angles += [(0 + 45 * j, -90 + 45 * i) for j in range(8)]
            angles = np.array(angles)
            d = np.abs(angles.reshape(26, 1, 2) - angles.reshape(1, 26, 2))
            d = np.sum(np.minimum(d, 360 - d), axis=2)
            ab = d == 45
            ab[0, -8::2] = True
            ab[-8::2, 0] = True
            ab[1, 2:10:2] = True
            ab[2:10:2, 1] = True
            sel = [np.argwhere(ab[i]).reshape(-1) for i in range(26)]
            K = max((len(s) for s in sel))
            idx = np.zeros((26, K), np.int32)
            msk = np.zeros((26, K), bool)
            for i, s in enumerate(sel):
                idx[i, :len(s)] = s
                msk[i, :len(s)] = True
            return (jnp.asarray(idx), jnp.asarray(msk))
        bt, c, h, w = x.shape
        B = bt // T
        L = h * w
        H = N_HEAD
        dh = c // H
        idx, msk = _neighbors()
        Kn = idx.shape[1]
        xt = x.reshape(B, T, c, L).transpose(0, 1, 3, 2)
        wq, wk, wv = jnp.split(w_in, 3, axis=0)
        bq, bk, bv = jnp.split(b_in, 3, axis=0)
        q = xt @ wq.T + bq
        kv = xt[:, idx].reshape(B, T, Kn * L, c)
        k = kv @ wk.T + bk
        v = kv @ wv.T + bv
        qh = q.reshape(B, T, L, H, dh)
        kh = k.reshape(B, T, Kn * L, H, dh)
        vh = v.reshape(B, T, Kn * L, H, dh)
        scores = jnp.einsum('btqhd,btkhd->bthqk', qh, kh) / math.sqrt(dh)
        key_bias = jnp.where(jnp.repeat(msk, L, axis=1), 0.0, -1000000000.0)
        scores = scores + key_bias[None, :, None, None, :]
        attn = jax.nn.softmax(scores, axis=-1)
        out = jnp.einsum('bthqk,btkhd->btqhd', attn, vh).reshape(B, T, L, c)
        out = out @ w_out.T + b_out
        return out.transpose(0, 1, 3, 2).reshape(bt, c, h, w)

    def _L1_conv_ref(x, w_down, w_up, w_right, w_left):
        import jax, jax.numpy as jnp
        import numpy as np
        K = 9
        PAD = K // 2

        def _conv1d(x, w):
            return jax.lax.conv_general_dilated(x, w, window_strides=(1,), padding=((PAD, PAD),), dimension_numbers=('NCH', 'OIH', 'NCH'))

        def _propagate(x, w, axis, reverse):
            xm = jnp.moveaxis(x, axis, 0)
            if reverse:
                xm = xm[::-1]

            def step(prev, cur):
                new = cur + jax.nn.relu(_conv1d(prev, w))
                return (new, new)
            _, outs = jax.lax.scan(step, xm[0], xm[1:])
            res = jnp.concatenate([xm[:1], outs], axis=0)
            if reverse:
                res = res[::-1]
            return jnp.moveaxis(res, 0, axis)
        x = _propagate(x, w_down, 2, False)
        x = _propagate(x, w_up, 2, True)
        x = _propagate(x, w_right, 3, False)
        x = _propagate(x, w_left, 3, True)
        return x

    def _gn(v, G=32, eps=1e-5):
        B_, C_, H_, W_ = v.shape
        g = v.reshape(B_, G, C_ // G, H_, W_)
        m = jnp.mean(g, axis=(2, 3, 4), keepdims=True)
        s = jnp.var(g, axis=(2, 3, 4), keepdims=True)
        return ((g - m) / jnp.sqrt(s + eps)).reshape(v.shape)

    def _ln_c(v, eps=1e-6):
        m = jnp.mean(v, axis=1, keepdims=True)
        s = jnp.var(v, axis=1, keepdims=True)
        return (v - m) / jnp.sqrt(s + eps)

    def _ln_t(v, eps=1e-5):
        m = jnp.mean(v, axis=-1, keepdims=True)
        s = jnp.var(v, axis=-1, keepdims=True)
        return (v - m) / jnp.sqrt(s + eps)

    def _to_tokens(v):
        B_, C_, H_, W_ = v.shape
        return v.reshape(B_, C_, H_ * W_).transpose(0, 2, 1)
    def _from_tokens(t, like):
        B_, C_, H_, W_ = like.shape
        return t.transpose(0, 2, 1).reshape(B_, C_, H_, W_)

    x = x + _L0_conv_ref(_gn(x), L0_conv_w_in, L0_conv_b_in, L0_conv_w_out, L0_conv_b_out)
    x = x + _L1_conv_ref(_gn(x), L1_conv_w_down, L1_conv_w_up, L1_conv_w_right, L1_conv_w_left)
    return x


_drawn_inputs = setup_inputs


def setup_inputs(seed=0):
    import zlib

    import numpy as np

    out = dict(_drawn_inputs(seed))
    spreads = {'L0_conv_b_in': (0.0, 0.36), 'L0_conv_b_out': (0.0, 0.454)}
    factors = {'L0_conv_w_in': 8.0}
    for name, (base, spread) in spreads.items():
        noise = np.random.default_rng([zlib.crc32(name.encode()), seed]).standard_normal(out[name].shape)
        drawn = base * np.exp(spread * noise) if base else spread * noise
        out[name] = jnp.asarray(drawn.astype(out[name].dtype))
    for name, factor in factors.items():
        out[name] = (out[name] * factor).astype(out[name].dtype)
    return out
```

```python
from contextlib import ExitStack

import numpy as np
import concourse.bass as bass
from concourse import mybir

F32 = mybir.dt.float32
F32R = mybir.dt.float32r
ACT = mybir.ActivationFunctionType
ALU = mybir.AluOpType
AX = mybir.AxisListType

IMAGES, C, SIDE = 104, 128, 16
L = SIDE * SIDE
T = 26
B = IMAGES // T
HEADS = 4
DH = C // HEADS
SCALE = float(DH) ** -0.5
GROUP = C // 32
TAPS = 9
STEPS = SIDE - 1
QT = L // 128
UNITS = HEADS * QT
PARTS = 3 * DH
ROWS = PARTS + 2

W_Q, W_K, W_V, W_O, AVG, IDENT, BIAS = 0, 128, 256, 384, 512, 640, 768
B_Q, B_K, B_V, B_O = BIAS, BIAS + 1, BIAS + 2, BIAS + 3
SMALL = BIAS + 4


def neighbours():
    angles = [(0, 90), (0, -90)]
    for i in range(1, 4):
        angles += [(45 * j, -90 + 45 * i) for j in range(8)]
    angles = np.array(angles)
    d = np.abs(angles.reshape(T, 1, 2) - angles.reshape(1, T, 2))
    d = np.sum(np.minimum(d, 360 - d), axis=2)
    near = d == 45
    near[0, -8::2] = True
    near[-8::2, 0] = True
    near[1, 2:10:2] = True
    near[2:10:2, 1] = True
    return [[int(j) for j in np.argwhere(near[i]).reshape(-1)] for i in range(T)]


NEAR = neighbours()
UNIT0 = [2 * sum(len(n) for n in NEAR[:t]) for t in range(T + 1)]
ALL_UNITS = UNIT0[T]
PAIRS = ALL_UNITS // 2
FIRST_SLOT, END_SLOT = 8 * (0 - 3) - 4, 8 * (T + 1) + 1

SHARED = {}
for _s in range(FIRST_SLOT, END_SLOT):
    for _kind, _off in (("q", 8 * 3 - 2), ("max", 8 - 5), ("out", -8 - 7)):
        _t, _r = divmod(_s + _off, 8)
        if _r == 0 and 0 <= _t < T:
            SHARED[_kind, _t] = len(SHARED)
SHARED_USES = len(SHARED)

X_RING, Q_RING, P_RING, S_RING = 7, 4, 4, 2
KGROUP = 4
KGROUPS = [min(KGROUP, T - g) for g in range(0, T, KGROUP)]
KG = len(KGROUPS)
KPAIRS = T // 2


def ring_total(n, ring, k):
    return (n - k + ring - 1) // ring


def build(nc, x, small, w_sweep, out):
    y_dram = nc.dram_tensor("y_after_attention", (IMAGES, C, L), F32, kind="Internal").ap()
    x_b = x.rearrange("(b t) c l -> b c t l", t=T)
    y_b = y_dram.rearrange("(b t) c l -> b c t l", t=T)
    x_all = x.rearrange("i c l -> c i l")
    y_all = y_dram.rearrange("i c l -> c i l")
    out_all = out.rearrange("i c l -> c i l")

    ctx = ExitStack()
    attention = ExitStack()
    with ctx:
        def sem(name):
            return ctx.enter_context(nc.semaphore(name))

        def sb(stack, name, shape, dt=F32):
            return stack.enter_context(nc.sbuf_tensor(name, shape, dt))

        cst = sb(ctx, "cst", [128, SMALL])
        stats = sb(ctx, "stats", [128, IMAGES, 6])
        work = sb(ctx, "work", [128, 5, IMAGES])
        norm = sb(ctx, "norm", [128, 2, IMAGES])
        out_bias = sb(ctx, "out_bias", [128, 1])
        ones = sb(ctx, "ones", [128, DH])

        kstack = sb(attention, "kstack", [128, T, HEADS, L], F32R)
        v = sb(attention, "v", [128, T, QT, C])
        probs = sb(attention, "probs", [128, P_RING, HEADS * L])
        sums = sb(attention, "sums", [128, S_RING, HEADS * L])
        qstack = sb(attention, "qstack", [128, Q_RING, HEADS, L], F32R)
        g_pair = sb(attention, "g_pair", [128, 2, 2 * L])
        x_t = sb(attention, "x_t", [128, X_RING, L])
        g_q = sb(attention, "g_q", [128, 2, L])
        q_hi = sb(attention, "q_hi", [128, 2, L], F32R)
        q_lo = sb(attention, "q_lo", [128, 2, L], F32R)
        row_max = sb(attention, "row_max", [128, 2, UNITS, 2])
        neg_max = sb(attention, "neg_max", [128, UNITS])
        max_parts = sb(attention, "max_parts", [128, 2, 2 * UNITS], F32R)
        max_rows = sb(attention, "max_rows", [2 * UNITS, 2, 128], F32R)
        recip = sb(attention, "recip", [128, L])
        attn = sb(attention, "attn", [128, 2, L])
        y_t = sb(attention, "y_t", [128, 2, L])
        norm_b = sb(attention, "norm_b", [128, 2, T])
        stats_b = sb(attention, "stats_b", [128, T, 6])
        k_hi = [probs[:, 2 * i, :].bitcast(F32R) for i in range(2)]
        k_lo = [probs[:, 2 * i + 1, :].bitcast(F32R) for i in range(2)]
        attention.close()

        PI = 2 * T
        xs = [sb(ctx, f"xs{p}", [128, PI, SIDE, SIDE]) for p in range(2)]
        w_raw = sb(ctx, "w_raw", [128, 2, TAPS * C])
        w_hi = sb(ctx, "w_hi", [128, 4, TAPS * C], F32R)
        w_lo = sb(ctx, "w_lo", [128, 4, TAPS * C], F32R)
        row_hi = sb(ctx, "row_hi", [128, 2, SIDE * T], F32R)
        row_lo = sb(ctx, "row_lo", [128, 2, SIDE * T], F32R)
        y_back = sb(ctx, "y_back", [128, 2, 4 * L])

        ps_t = [ctx.enter_context(nc.psum_tensor(f"ps_t{i}", [128, 512], F32)) for i in range(3)]
        ps_m = [ctx.enter_context(nc.psum_tensor(f"ps_m{i}", [128, 512], F32)) for i in range(2)]
        ps_o = [ctx.enter_context(nc.psum_tensor(f"ps_o{i}", [128, 512], F32)) for i in range(2)]
        ps_x = ctx.enter_context(nc.psum_tensor("ps_x", [128, 512], F32))

        s_small = sem("small_loaded")
        s_const = sem("constants_set")
        s_pre = [sem(f"prepass_x_loaded{i}") for i in range(P_RING)]
        s_read = sem("prepass_x_read")
        s_link = sem("dve_step")
        s_mean = sem("channel_means_made")
        s_var = sem("channel_variances_made")
        s_veps = sem("group_variance_plus_eps_made")
        s_ob = sem("value_bias_projected")
        s_ob2 = sem("output_bias_made")
        s_avg = sem("group_average_made")
        s_rt = sem("square_root_made")
        s_start = sem("sample_may_start")
        s_normb = sem("norm_of_sample_ready")
        s_xk = [sem(f"key_x_loaded{i}") for i in range(2)]
        s_g = sem("key_g_made")
        s_kp = sem("keys_and_values_projected")
        s_khi = sem("key_hi_made")
        s_klo = sem("key_lo_made")
        s_v = sem("values_copied")
        s_ks = [sem(f"keys_stacked{i}") for i in range(2)]
        s_xt = [sem(f"x_t_loaded{i}") for i in range(X_RING)]
        s_gq = sem("query_g_made")
        s_qp = sem("query_projected")
        s_qhi = sem("query_hi_made")
        s_qlo = sem("query_lo_made")
        s_qs = [sem(f"query_stacked{i}") for i in range(Q_RING)]
        s_ms = [sem(f"row_scores_made{i}") for i in range(2)]
        s_mr = [sem(f"row_max_made{i}") for i in range(2)]
        s_neg = sem("negative_max_made")
        s_mhi = sem("max_hi_made")
        s_mp = sem("max_parts_made")
        s_mt = sem("max_transposed")
        s_mc = sem("max_rows_copied")
        s_mk = [sem(f"max_stacked{i}") for i in range(2)]
        s_t = sem("scores_made")
        s_e = sem("exp_made")
        s_pv = sem("values_product_made")
        s_ps = sem("pair_summed")
        s_d = sem("row_sums_made")
        s_rc = sem("row_sums_inverted")
        s_n = sem("attention_divided")
        s_op = sem("output_projected")
        s_y = sem("y_made")
        s_st = sem("y_stats_made")
        s_ys = [sem(f"y_stored{i}") for i in range(2)]
        s_w = [sem(f"sweep_w_loaded{i}") for i in range(2)]
        s_wsp = sem("sweep_w_split")
        s_whi = sem("sweep_w_hi_made")
        s_yl = [sem(f"first_pair_y_loaded{i}") for i in range(2 * T // 4)]
        s_yl2 = sem("second_pair_y_loaded")
        s_xn = [sem(f"pair_normalised{i}") for i in range(2)]
        s_cv = [sem(f"conv_made{i}") for i in range(2)]
        s_new = [sem(f"new_row_made{i}") for i in range(2)]
        s_hi = [sem(f"row_hi_made{i}") for i in range(2)]
        s_lo = [sem(f"row_lo_made{i}") for i in range(2)]
        s_yb = [sem(f"y_reloaded{i}") for i in range(2)]
        s_yp = sem("pair_b_y_reloaded")
        s_fa = sem("first_pair_added")
        s_fb = sem("second_pair_added")
        s_out = sem("out_stored")

        PRE = IMAGES // 4
        PG = PI // 4
        PER_KS = [12 * 16 * ring_total(KG, 2, i) for i in range(2)]
        FINAL_SPLITS = 62

        block = ctx.enter_context(nc.Block())

        def stack_keys(queue, k, n, h, parts):
            for part in parts:
                src = (k_hi, k_lo, k_hi)[part][k % 2]
                queue.dma_start(
                    kstack[DH * part:DH * part + DH, KGROUP * k:KGROUP * k + n, h, :].bitcast(F32),
                    src[DH * h:DH * h + DH, 0:n * L].bitcast(F32).rearrange("c (i l) -> c i l", l=L)
                ).then_inc(s_ks[k % 2], 16)

        def store(queue, pair, k, added):
            queue.wait_ge(added, k + 1)
            queue.dma_start(out_all[:, pair * PI + 4 * k:pair * PI + 4 * k + 4, :],
                            xs[pair][:, 4 * k:4 * k + 4, :, :].rearrange("c i h w -> c i (h w)")
                            ).then_inc(s_out, 16)

        def parts_of(row, c):
            return row[:, c, :].rearrange("c (p i) -> c p i", i=T)

        def place(d, j):
            return j if d % 2 == 0 else j * -1 + STEPS

        def line(xp, c, d, at):
            one = xp[:, c * T:c * T + T, bass.ds(at, 1), :] if d < 2 else xp[:, c * T:c * T + T, :, bass.ds(at, 1)]
            return one.rearrange("c i a w -> c (a w) i") if d < 2 else one.rearrange("c i h a -> c (h a) i")

        @block.sync
        def _(sp):
            sp.dma_start(cst[:, :], small).then_inc(s_small, 16)
            for n in range(PRE):
                if n >= P_RING:
                    sp.wait_ge(s_read, n - P_RING + 1)
                sp.dma_start(probs[:, n % P_RING, :].rearrange("c (i l) -> c i l", l=L),
                             x_all[:, 4 * n:4 * n + 4, :]).then_inc(s_pre[n % P_RING], 16)

            with sp.Fori(0, B) as b:
                sp.wait_ge(s_start, b + 1)
                xb = x_b[b]

                def load_keys_x(k):
                    n = KGROUPS[k]
                    sp.dma_start(sums[:, k % 2, 0:n * L].rearrange("c (i l) -> c i l", l=L),
                                 xb[:, KGROUP * k:KGROUP * k + n, :]).then_inc(s_xk[k % 2], 16)

                load_keys_x(0)
                load_keys_x(1)
                for k in range(KG):
                    last_pair = (KGROUP * k + KGROUPS[k]) // 2
                    if k + 2 < KG:
                        sp.wait_ge(s_g, b * KPAIRS + last_pair)
                        load_keys_x(k + 2)
                    sp.wait_ge(s_klo, b * KPAIRS + last_pair)
                    n = KGROUPS[k]
                    for h in range(2):
                        stack_keys(sp, k, n, h, (0, 1, 2))

                for s in range(FIRST_SLOT, END_SLOT):
                    t, r = divmod(s + 24 - 3, 8)
                    if r == 0 and 0 <= t < T:
                        sp.wait_ge(s_qlo, b * T + t + 1)
                        for h in range(HEADS):
                            for part, src in enumerate((q_hi, q_hi, q_lo)):
                                sp.dma_start(qstack[DH * part:DH * part + DH, t % Q_RING, h, :].bitcast(F32),
                                             src[DH * h:DH * h + DH, t % 2, :].bitcast(F32)
                                             ).then_inc(s_qs[t % Q_RING], 16)

            sp.wait_ge(s_start, B + 1)
            for i in range(2):
                sp.wait_ge(s_ys[i], 16 * B * ring_total(T, 2, i))
            for d in range(2):
                sp.dma_start(w_raw[:, d, :], w_sweep[:, d, :]).then_inc(s_w[d], 16)
            for k in range(PG):
                sp.dma_start(xs[0][:, 4 * k:4 * k + 4, :, :].rearrange("c i h w -> c i (h w)"),
                             y_all[:, 4 * k:4 * k + 4, :]).then_inc(s_yl[k], 16)
            for d in range(2, 4):
                sp.wait_ge(s_wsp, d - 1)
                sp.dma_start(w_raw[:, d - 2, :], w_sweep[:, d, :]).then_inc(s_w[d - 2], 16)
            for k in range(PG):
                sp.dma_start(xs[1][:, 4 * k:4 * k + 4, :, :].rearrange("c i h w -> c i (h w)"),
                             y_all[:, PI + 4 * k:PI + 4 * k + 4, :]).then_inc(s_yl2, 16)
            for k in range(PG):
                if k >= 2:
                    sp.wait_ge(s_fa, k - 1)
                sp.dma_start(y_back[:, k % 2, :].rearrange("c (i l) -> c i l", l=L),
                             y_all[:, 4 * k:4 * k + 4, :]).then_inc(s_yb[k % 2], 16)
                if k >= 1:
                    store(sp, 0, k - 1, s_fa)
            store(sp, 0, PG - 1, s_fa)
            sp.wait_ge(s_out, 16 * PG)
            sp.dma_start(xs[0][:, :, :, :].rearrange("c i h w -> c i (h w)"),
                         y_all[:, PI:2 * PI, :]).then_inc(s_yp, 16)
            for k in range(PG):
                store(sp, 1, k, s_fb)
            sp.wait_ge(s_out, 16 * 2 * PG)

        @block.gpsimd
        def _(pool):
            pool.memset(ones[:, :], 1.0).then_inc(s_const, 1)
            pool.wait_ge(s_const, 1)
            pool.memset(kstack[PARTS:ROWS, :, :, :].bitcast(F32), 1.0).then_inc(s_const, 1)
            with pool.Fori(0, B) as b:
                for p in range(PAIRS):
                    pool.wait_ge(s_e, b * 2 * ALL_UNITS + 4 * p + 4)
                    if p >= S_RING:
                        pool.wait_ge(s_d, b * PAIRS + p - S_RING + 1)
                    nc.gpsimd.tensor_tensor(sums[:, p % S_RING, :], probs[:, 2 * p % P_RING, :],
                                            probs[:, (2 * p + 1) % P_RING, :], ALU.add).then_inc(s_ps, 1)
            pool.wait_ge(s_start, B + 2)
            pool.wait_ge(s_yl2, 16 * PG)
            for i in range(PI):
                last = nc.gpsimd.tensor_scalar(xs[1][:, i, :, :], xs[1][:, i, :, :],
                                               norm[:, 0, PI + i:PI + i + 1], norm[:, 1, PI + i:PI + i + 1],
                                               ALU.mult, ALU.add)
            last.then_inc(s_xn[1], 1)
            for c in range(2):
                pool.wait_ge(s_lo[c], FINAL_SPLITS)
            for k in range(PG):
                pool.wait_ge(s_yb[k % 2], 16 * (k // 2 + 1))
                part = xs[0][:, 4 * k:4 * k + 4, :, :].rearrange("c i h w -> c (i h w)")
                nc.gpsimd.tensor_tensor(part, part, y_back[:, k % 2, :], ALU.add).then_inc(s_fa, 1)

        @block.scalar
        def _(act):
            act.wait_ge(s_small, 16)
            act.wait_ge(s_veps, 1)
            nc.scalar.activation(work[:, 3, :], work[:, 2, :], ACT.Sqrt).then_inc(s_rt, 1)
            with act.Fori(0, B) as b:
                act.wait_ge(s_start, b + 1)
                xb = x_b[b]
                for p in range(KPAIRS):
                    k, j = divmod(p, 2)
                    act.wait_ge(s_kp, b * 2 * KPAIRS + 2 * p + 1)
                    if k >= 2 and j == 0:
                        act.wait_ge(s_ks[k % 2], b * PER_KS[k % 2] + 12 * 16 * (k // 2))
                    nc.scalar.activation(k_hi[k % 2][:, 512 * j:512 * j + 512], ps_t[p % 2][:, :], ACT.Identity,
                                         bias=cst[:, B_K:B_K + 1]).then_inc(s_khi, 1)
                    act.wait_ge(s_kp, b * 2 * KPAIRS + 2 * p + 2)
                    nc.scalar.activation(v[:, 2 * p:2 * p + 2, :, :].rearrange("p i k c -> p (i k c)"),
                                         ps_m[p % 2][:, :], ACT.Copy).then_inc(s_v, 1)
                    if j == 1 or p == KPAIRS - 1:
                        act.wait_ge(s_klo, b * KPAIRS + p + 1)
                        for h in range(2, HEADS):
                            stack_keys(act, k, KGROUPS[k], h, (0, 1, 2))

                for s in range(FIRST_SLOT, END_SLOT):
                    t, r = divmod(s + 24 + 4, 8)
                    if r == 0 and 0 <= t < T:
                        if t >= X_RING:
                            act.wait_ge(s_y, b * T + t - X_RING + 1)
                        act.dma_start(x_t[:, t % X_RING, :], xb[:, t, :]).then_inc(s_xt[t % X_RING], 16)
                    t, u = divmod(s, 8)
                    if 0 <= t < T and u < 2 * len(NEAR[t]):
                        n = UNIT0[t] + u
                        for half in range(2):
                            act.wait_ge(s_t, b * 2 * ALL_UNITS + 2 * n + half + 1)
                            if half == 0 and n >= P_RING:
                                act.wait_ge(s_pv, b * ALL_UNITS + n - P_RING + 1)
                                act.wait_ge(s_ps, b * PAIRS + (n - P_RING) // 2 + 1)
                            nc.scalar.activation(probs[:, n % P_RING, 512 * half:512 * half + 512],
                                                 ps_t[(2 * n + half) % 3][:, :], ACT.Exp,
                                                 scale=SCALE).then_inc(s_e, 1)
                    t, r = divmod(s + 24 - 2, 8)
                    if r == 0 and 0 <= t < T:
                        act.wait_ge(s_qp, b * T + t + 1)
                        if t >= 2:
                            act.wait_ge(s_qs[(t - 2) % Q_RING], b * 192 * ring_total(T, Q_RING, (t - 2) % Q_RING)
                                        + 192 * ((t - 2) // Q_RING + 1))
                        nc.scalar.activation(q_hi[:, t % 2, :], ps_x[:, 0:L], ACT.Identity,
                                             bias=cst[:, B_Q:B_Q + 1]).then_inc(s_qhi, 1)
                    t, r = divmod(s + 8 - 6, 8)
                    if r == 0 and 0 <= t < T:
                        act.wait_ge(s_mc, b * T + t + 1)
                        for part in range(2):
                            act.dma_start(
                                qstack[PARTS + part:PARTS + part + 1, t % Q_RING, :, :].bitcast(F32)
                                .rearrange("p h (k l) -> p (h k) l", l=128),
                                max_rows[UNITS * part:UNITS * part + UNITS, t % 2, :].bitcast(F32)
                            ).then_inc(s_mk[t % 2], 16)
                    t, r = divmod(s - 16 - 1, 8)
                    if (r == 0 and 0 <= t < T) or s == END_SLOT - 1:
                        t = min(t, T - 1) if r == 0 else T - 1
                        act.wait_ge(s_y, b * T + t + 1)
                        act.dma_start(y_b[b][:, t, :], y_t[:, t % 2, :]).then_inc(s_ys[t % 2], 16)

            act.wait_ge(s_veps, 2)
            nc.scalar.activation(work[:, 3, :], work[:, 2, :], ACT.Sqrt).then_inc(s_rt, 1)
            for pair in range(2):
                done, splits = 4 * STEPS * pair, FINAL_SPLITS * pair
                for d in range(4):
                    if d % 2 == 0:
                        if d == 0:
                            act.wait_ge(s_xn[pair], 1)
                        for c in range(2):
                            if splits:
                                act.wait_ge(s_lo[c], splits)
                            nc.scalar.activation(parts_of(row_hi, c), line(xs[pair], c, d, 0),
                                                 ACT.Copy).then_inc(s_hi[c], 1)
                        splits += 1
                    with act.Fori(1, STEPS + 1) as j:
                        for c in range(2):
                            act.wait_ge(s_new[c], j + done)
                            nc.scalar.activation(parts_of(row_hi, c), line(xs[pair], c, d, place(d, j)),
                                                 ACT.Copy).then_inc(s_hi[c], 1)
                    done += STEPS
                    splits += STEPS

        @block.vector
        def _(dve):
            vec = nc.vector
            links = [0]

            def link(ins):
                links[0] += 1
                ins.then_inc(s_link, 1)
                dve.wait_ge(s_link, links[0])

            def norm_tables(which):
                mean, var, t2, root, scratch = (work[:, i, :] for i in range(5))
                link(vec.tensor_tensor(t2, stats[:, :, 1], stats[:, :, 4], ALU.subtract))
                link(vec.tensor_scalar(scratch, t2, 0.5, None, ALU.mult))
                link(vec.tensor_tensor(t2, scratch, scratch, ALU.mult))
                link(vec.tensor_tensor(var, stats[:, :, 2], stats[:, :, 5], ALU.add))
                link(vec.scalar_tensor_tensor(var, var, 1.0 / L, t2, ALU.mult, ALU.add))
                link(vec.tensor_tensor(scratch, stats[:, :, 1], stats[:, :, 4], ALU.add))
                vec.tensor_scalar(mean, scratch, 0.5, None, ALU.mult).then_inc(s_mean, 1)
                dve.wait_ge(s_avg, 2 * which + 1)
                link(vec.tensor_tensor(t2, mean, ps_x[:, 0:IMAGES], ALU.subtract))
                link(vec.tensor_tensor(scratch, t2, t2, ALU.mult))
                link(vec.tensor_scalar(norm[:, 1, :], ps_x[:, 0:IMAGES], -1.0, None, ALU.mult))
                vec.tensor_tensor(var, scratch, var, ALU.add).then_inc(s_var, 1)
                dve.wait_ge(s_avg, 2 * which + 2)
                vec.tensor_scalar(t2, ps_x[:, 128:128 + IMAGES], 1e-5, None, ALU.add).then_inc(s_veps, 1)
                dve.wait_ge(s_rt, which + 1)
                scale = norm[:, 0, :]
                link(vec.reciprocal(scale, root))
                link(vec.tensor_tensor(scratch, scale, scale, ALU.mult))
                link(vec.tensor_tensor(scratch, scratch, t2, ALU.mult))
                link(vec.tensor_scalar(scratch, scratch, -0.5, 1.5, ALU.mult, ALU.add))
                link(vec.tensor_tensor(scale, scale, scratch, ALU.mult))
                return vec.tensor_tensor(norm[:, 1, :], norm[:, 1, :], scale, ALU.mult)

            for n in range(PRE):
                dve.wait_ge(s_pre[n % P_RING], 16 * (n // P_RING + 1))
                for i in range(4):
                    last = vec.bn_stats(stats[:, 4 * n + i, :], probs[:, n % P_RING, L * i:L * i + L])
                last.then_inc(s_read, 1)
            dve.wait_ge(s_read, PRE)
            dve.wait_ge(s_small, 16)
            dve.wait_ge(s_ob, 1)
            vec.tensor_scalar(out_bias[:, :], ps_x[:, 256:257], cst[:, B_O:B_O + 1], None, ALU.add).then_inc(s_ob2, 1)
            norm_tables(0).then_inc(s_start, 1)

            with dve.Fori(0, B) as b:
                dve.wait_ge(s_start, b + 1)
                vec.tensor_copy(norm_b[:, :, :], norm[:, :, bass.ds(b * T, T)]).then_inc(s_normb, 1)
                dve.wait_ge(s_normb, b + 1)

                def key_g(p):
                    k, j = divmod(p, 2)
                    if j == 0:
                        dve.wait_ge(s_xk[k % 2], b * 16 * ring_total(KG, 2, k % 2) + 16 * (k // 2 + 1))
                    if p >= 2:
                        dve.wait_ge(s_kp, b * 2 * KPAIRS + 2 * p - 2)
                    for i in range(2):
                        m = 2 * p + i
                        last = vec.tensor_scalar(g_pair[:, p % 2, L * i:L * i + L],
                                                 sums[:, k % 2, L * (2 * j + i):L * (2 * j + i) + L],
                                                 norm_b[:, 0, m:m + 1], norm_b[:, 1, m:m + 1], ALU.mult, ALU.add)
                    last.then_inc(s_g, 1)

                key_g(0)
                for p in range(KPAIRS):
                    if p + 1 < KPAIRS:
                        key_g(p + 1)
                    k, j = divmod(p, 2)
                    dve.wait_ge(s_khi, b * KPAIRS + p + 1)
                    vec.scalar_tensor_tensor(k_lo[k % 2][:, 512 * j:512 * j + 512], ps_t[p % 2][:, :],
                                             cst[:, B_K:B_K + 1],
                                             k_hi[k % 2][:, 512 * j:512 * j + 512].bitcast(F32),
                                             ALU.add, ALU.subtract).then_inc(s_klo, 1)

                for s in range(FIRST_SLOT, END_SLOT):
                    t, r = divmod(s - 16, 8)
                    if r == 0 and 0 <= t < T:
                        dve.wait_ge(s_op, b * T + t + 1)
                        if t >= 2:
                            dve.wait_ge(s_ys[t % 2], b * 16 * ring_total(T, 2, t % 2) + 16 * (t // 2))
                        vec.scalar_tensor_tensor(y_t[:, t % 2, :], ps_x[:, 0:L], out_bias[:, 0:1],
                                                 x_t[:, t % X_RING, :], ALU.add, ALU.add).then_inc(s_y, 1)
                        dve.wait_ge(s_y, b * T + t + 1)
                        vec.bn_stats(stats_b[:, t, :], y_t[:, t % 2, :]).then_inc(s_st, 1)
                    t, w = divmod(s + 12, 8)
                    if 0 <= t < T:
                        for half in range(2):
                            n = len(NEAR[t][2 * half:2 * half + 2])
                            dve.wait_ge(s_ms[half], b * T * UNITS + UNITS * t + w + 1)
                            vec.tensor_reduce(row_max[:, t % 2, w, half:half + 1], ps_m[half][:, 0:n * L],
                                              AX.X, ALU.max).then_inc(s_mr[half], 1)
                        if w == UNITS - 1:
                            for half in range(2):
                                dve.wait_ge(s_mr[half], b * T * UNITS + UNITS * (t + 1))
                            vec.tensor_reduce(neg_max[:, :], row_max[:, t % 2, :, :], AX.X, ALU.max,
                                              negate=True).then_inc(s_neg, 1)
                            dve.wait_ge(s_neg, b * T + t + 1)
                            if t >= 2:
                                dve.wait_ge(s_mt, b * T + t - 1)
                            vec.tensor_copy(max_parts[:, t % 2, 0:UNITS], neg_max[:, :]).then_inc(s_mhi, 1)
                            dve.wait_ge(s_mhi, b * T + t + 1)
                            vec.tensor_tensor(max_parts[:, t % 2, UNITS:2 * UNITS], neg_max[:, :],
                                              max_parts[:, t % 2, 0:UNITS].bitcast(F32),
                                              ALU.subtract).then_inc(s_mp, 1)
                    t, r = divmod(s + 24 - 1, 8)
                    if r == 0 and 0 <= t < T:
                        dve.wait_ge(s_xt[t % X_RING], b * 16 * ring_total(T, X_RING, t % X_RING)
                                    + 16 * (t // X_RING + 1))
                        if t >= 2:
                            dve.wait_ge(s_qp, b * T + t - 1)
                        vec.tensor_scalar(g_q[:, t % 2, :], x_t[:, t % X_RING, :], norm_b[:, 0, t:t + 1],
                                          norm_b[:, 1, t:t + 1], ALU.mult, ALU.add).then_inc(s_gq, 1)
                    t, r = divmod(s + 24 - 3, 8)
                    if r == 0 and 0 <= t < T:
                        dve.wait_ge(s_qhi, b * T + t + 1)
                        vec.scalar_tensor_tensor(q_lo[:, t % 2, :], ps_x[:, 0:L], cst[:, B_Q:B_Q + 1],
                                                 q_hi[:, t % 2, :].bitcast(F32),
                                                 ALU.add, ALU.subtract).then_inc(s_qlo, 1)
                    t, r = divmod(s - 8 - 4, 8)
                    if r == 0 and 0 <= t < T:
                        dve.wait_ge(s_d, b * PAIRS + UNIT0[t + 1] // 2)
                        if t >= 1:
                            dve.wait_ge(s_n, b * T + t)
                        vec.reciprocal(recip[:, :], ps_o[t % 2][:, L:2 * L]).then_inc(s_rc, 1)
                        dve.wait_ge(s_rc, b * T + t + 1)
                        if t >= 2:
                            dve.wait_ge(s_op, b * T + t - 1)
                        vec.tensor_tensor(attn[:, t % 2, :], ps_o[t % 2][:, 0:L], recip[:, :],
                                          ALU.mult).then_inc(s_n, 1)
                    t, r = divmod(s + 8 - 6, 8)
                    if r == 0 and 0 <= t < T:
                        dve.wait_ge(s_mt, b * T + t + 1)
                        if t >= 2:
                            dve.wait_ge(s_mk[t % 2], b * 32 * ring_total(T, 2, t % 2) + 32 * (t // 2))
                        vec.tensor_copy(max_rows[:, t % 2, :], ps_x[0:2 * UNITS, 0:128]).then_inc(s_mc, 1)
                dve.wait_ge(s_st, b * T + T)
                for i in range(2):
                    dve.wait_ge(s_ys[i], b * 16 * ring_total(T, 2, i) + 16 * ring_total(T, 2, i))
                vec.tensor_copy(stats[:, bass.ds(b * T, T), :], stats_b[:, :, :]).then_inc(s_start, 1)

            dve.wait_ge(s_start, B + 1)
            norm_tables(1).then_inc(s_start, 1)
            dve.wait_ge(s_start, B + 2)

            def split_weights(d):
                dve.wait_ge(s_w[d % 2], 16 * (d // 2 + 1))
                vec.tensor_copy(w_hi[:, d, :], w_raw[:, d % 2, :]).then_inc(s_whi, 1)
                dve.wait_ge(s_whi, d + 1)
                vec.tensor_tensor(w_lo[:, d, :], w_raw[:, d % 2, :], w_hi[:, d, :].bitcast(F32),
                                  ALU.subtract).then_inc(s_wsp, 1)

            split_weights(0)
            split_weights(1)
            for k in range(PG):
                dve.wait_ge(s_yl[k], 16)
                for i in range(4 * k, 4 * k + 4):
                    last = vec.tensor_scalar(xs[0][:, i, :, :], xs[0][:, i, :, :],
                                             norm[:, 0, i:i + 1], norm[:, 1, i:i + 1], ALU.mult, ALU.add)
            last.then_inc(s_xn[0], 1)
            for pair in range(2):
                done, splits = 4 * STEPS * pair, FINAL_SPLITS * pair

                def row_parts(c, d, at, count):
                    dve.wait_ge(s_hi[c], count)
                    vec.tensor_tensor(parts_of(row_lo, c), line(xs[pair], c, d, at),
                                      parts_of(row_hi, c).bitcast(F32), ALU.subtract).then_inc(s_lo[c], 1)

                for d in range(4):
                    if d % 2 == 0:
                        splits += 1
                        for c in range(2):
                            row_parts(c, d, 0, splits)
                    with dve.Fori(1, STEPS + 1) as j:
                        at = dve.snap(place(d, j))
                        for c in range(2):
                            dve.wait_ge(s_cv[c], j + done)
                            now = line(xs[pair], c, d, at)
                            vec.scalar_tensor_tensor(now, ps_t[c][:, 0:SIDE * T].rearrange("c (p i) -> c p i", i=T),
                                                     0.0, now, ALU.max, ALU.add).then_inc(s_new[c], 1)
                            row_parts(c, d, at, j + splits)
                    if pair == 0 and d == 0:
                        split_weights(2)
                        split_weights(3)
                    done += STEPS
                    splits += STEPS
            for c in range(2):
                dve.wait_ge(s_lo[c], 2 * FINAL_SPLITS)
            dve.wait_ge(s_yp, 16)
            for k in range(PG):
                part = xs[1][:, 4 * k:4 * k + 4, :, :].rearrange("c i h w -> c (i h w)")
                back = xs[0][:, 4 * k:4 * k + 4, :, :].rearrange("c i h w -> c (i h w)")
                vec.tensor_tensor(part, part, back, ALU.add).then_inc(s_fb, 1)

        @block.tensor
        def _(pe):
            mm = nc.tensor.matmul

            def group_averages(which):
                pe.wait_ge(s_mean, which + 1)
                mm(ps_x[:, 0:IMAGES], cst[:, AVG:AVG + 128], work[:, 0, :], start=True, stop=True).then_inc(s_avg, 1)
                pe.wait_ge(s_var, which + 1)
                mm(ps_x[:, 128:128 + IMAGES], cst[:, AVG:AVG + 128], work[:, 1, :],
                   start=True, stop=True).then_inc(s_avg, 1)

            pe.wait_ge(s_small, 16)
            mm(ps_x[:, 256:257], cst[:, W_O:W_O + 128], cst[:, B_V:B_V + 1], start=True, stop=True).then_inc(s_ob, 1)
            pe.wait_ge(s_ob2, 1)
            group_averages(0)
            pe.wait_ge(s_const, 2)

            with pe.Fori(0, B) as b:
                pe.wait_ge(s_start, b + 1)
                for p in range(KPAIRS):
                    pe.wait_ge(s_g, b * KPAIRS + p + 1)
                    if p >= 2:
                        pe.wait_ge(s_klo, b * KPAIRS + p - 1)
                    mm(ps_t[p % 2][:, :], cst[:, W_K:W_K + 128], g_pair[:, p % 2, :],
                       start=True, stop=True).then_inc(s_kp, 1)
                    if p >= 2:
                        pe.wait_ge(s_v, b * KPAIRS + p - 1)
                    for i in range(2 * QT):
                        last = mm(ps_m[p % 2][:, 128 * i:128 * i + 128], g_pair[:, p % 2, 128 * i:128 * i + 128],
                                  cst[:, W_V:W_V + 128], start=True, stop=True)
                    last.then_inc(s_kp, 1)
                pe.wait_ge(s_v, b * KPAIRS + KPAIRS)
                pe.wait_ge(s_klo, b * KPAIRS + KPAIRS)

                def shared_bank(kind, t):
                    n = SHARED[kind, t]
                    if n:
                        (before, tb), = [u for u in SHARED if SHARED[u] == n - 1]
                        pe.wait_ge({"q": s_qlo, "max": s_mc, "out": s_y}[before], b * T + tb + 1)

                for s in range(FIRST_SLOT, END_SLOT):
                    t, w = divmod(s + 12, 8)
                    if 0 <= t < T:
                        h, qt = divmod(w, QT)
                        if (t, w) == (0, 0):
                            for i in range(2):
                                pe.wait_ge(s_ks[i], b * PER_KS[i] + PER_KS[i])
                        if w == 0:
                            pe.wait_ge(s_qs[t % Q_RING], b * 192 * ring_total(T, Q_RING, t % Q_RING)
                                       + 192 * (t // Q_RING + 1))
                        for half in range(2):
                            if UNITS * t + w:
                                pe.wait_ge(s_mr[half], b * T * UNITS + UNITS * t + w)
                            for i, m in enumerate(NEAR[t][2 * half:2 * half + 2]):
                                last = mm(ps_m[half][:, L * i:L * i + L],
                                          qstack[0:PARTS, t % Q_RING, h, 128 * qt:128 * qt + 128],
                                          kstack[0:PARTS, m, h, :], start=True, stop=True)
                            last.then_inc(s_ms[half], 1)
                    t, u = divmod(s, 8)
                    if 0 <= t < T and u < 2 * len(NEAR[t]):
                        n = UNIT0[t] + u
                        m, kt = NEAR[t][u // 2], u % 2
                        if u == 0:
                            pe.wait_ge(s_mk[t % 2], b * 32 * ring_total(T, 2, t % 2) + 32 * (t // 2 + 1))
                        for half in range(2):
                            if 2 * n + half >= 3:
                                pe.wait_ge(s_e, b * 2 * ALL_UNITS + 2 * n + half - 2)
                            for i in range(2):
                                last = mm(ps_t[(2 * n + half) % 3][:, L * i:L * i + L],
                                          kstack[0:ROWS, m, 2 * half + i, 128 * kt:128 * kt + 128],
                                          qstack[0:ROWS, t % Q_RING, 2 * half + i, :], start=True, stop=True)
                            last.then_inc(s_t, 1)
                    t, u = divmod(s - 1, 8)
                    if 0 <= t < T and u < 2 * len(NEAR[t]):
                        n = UNIT0[t] + u
                        m, kt = NEAR[t][u // 2], u % 2
                        if u == 0 and t >= 2:
                            pe.wait_ge(s_n, b * T + t - 1)
                        pe.wait_ge(s_e, b * 2 * ALL_UNITS + 2 * n + 2)
                        for h in range(HEADS):
                            last = mm(ps_o[t % 2][DH * h:DH * h + DH, 0:L], v[:, m, kt, DH * h:DH * h + DH],
                                      probs[:, n % P_RING, L * h:L * h + L],
                                      start=(u == 0), stop=(u == 2 * len(NEAR[t]) - 1), skip_group_check=True)
                        last.then_inc(s_pv, 1)
                    t, r = divmod(s - 4, 8)
                    if r % 2 == 0 and 0 <= t < T and r // 2 < len(NEAR[t]):
                        n = UNIT0[t] // 2 + r // 2
                        pe.wait_ge(s_ps, b * PAIRS + n + 1)
                        for h in range(HEADS):
                            last = mm(ps_o[t % 2][DH * h:DH * h + DH, L:2 * L], ones[:, :],
                                      sums[:, n % S_RING, L * h:L * h + L],
                                      start=False, stop=(r // 2 == len(NEAR[t]) - 1), skip_group_check=True)
                        last.then_inc(s_d, 1)
                    t, r = divmod(s + 24 - 2, 8)
                    if r == 0 and 0 <= t < T:
                        shared_bank("q", t)
                        pe.wait_ge(s_gq, b * T + t + 1)
                        mm(ps_x[:, 0:L], cst[:, W_Q:W_Q + 128], g_q[:, t % 2, :], start=True, stop=True).then_inc(s_qp, 1)
                    t, r = divmod(s + 8 - 5, 8)
                    if r == 0 and 0 <= t < T:
                        shared_bank("max", t)
                        pe.wait_ge(s_mp, b * T + t + 1)
                        mm(ps_x[0:2 * UNITS, 0:128], max_parts[:, t % 2, :].bitcast(F32),
                           cst[:, IDENT:IDENT + 128], start=True, stop=True).then_inc(s_mt, 1)
                    t, r = divmod(s - 8 - 7, 8)
                    if r == 0 and 0 <= t < T:
                        shared_bank("out", t)
                        pe.wait_ge(s_n, b * T + t + 1)
                        mm(ps_x[:, 0:L], cst[:, W_O:W_O + 128], attn[:, t % 2, :], start=True, stop=True).then_inc(s_op, 1)

            group_averages(1)
            for pair in range(2):
                done, splits = 0, FINAL_SPLITS * pair
                for d in range(4):
                    if pair == 0:
                        pe.wait_ge(s_wsp, d + 1)
                    if d % 2 == 0:
                        splits += 1
                    with pe.Fori(0, STEPS) as j:
                        for c in range(2):
                            pe.wait_ge(s_lo[c], j + splits)
                            taps = sorted(range(TAPS), key=lambda k: abs(k - TAPS // 2))
                            for k in taps:
                                shift = k - TAPS // 2
                                lo, hi = max(0, -shift) * T, (SIDE - max(0, shift)) * T
                                for w, row in ((w_hi, row_hi), (w_lo, row_hi), (w_hi, row_lo)):
                                    last = mm(ps_t[c][:, lo:hi], w[:, d, C * k:C * k + C],
                                              row[:, c, lo + shift * T:hi + shift * T],
                                              start=(k == taps[0] and w is w_hi and row is row_hi),
                                              stop=(k == taps[-1] and row is row_lo))
                            last.then_inc(s_cv[c], 1)
                    splits += STEPS


def kernel(x, L0_conv_w_in, L0_conv_b_in, L0_conv_w_out, L0_conv_b_out,
           L1_conv_w_down, L1_conv_w_up, L1_conv_w_right, L1_conv_w_left):
    import concourse.bacc as _bacc
    from concourse.bass_utils import run_bass_kernel_spmd as _run

    w_in = np.asarray(L0_conv_w_in)
    average = np.kron(np.eye(C // GROUP, dtype=np.float32), np.full((GROUP, GROUP), 1.0 / GROUP, np.float32))
    small = np.concatenate(
        [w_in[C * i:C * i + C].T for i in range(3)]
        + [np.asarray(L0_conv_w_out).T, average, np.eye(128, dtype=np.float32),
           np.asarray(L0_conv_b_in).reshape(3, C).T, np.asarray(L0_conv_b_out).reshape(C, 1)], axis=1)
    sweeps = np.stack([np.asarray(w) for w in (L1_conv_w_down, L1_conv_w_up, L1_conv_w_right, L1_conv_w_left)])
    arrays = {
        "x_dram": np.ascontiguousarray(np.asarray(x).reshape(IMAGES, C, L)),
        "small_dram": np.ascontiguousarray(small),
        "sweep_dram": np.ascontiguousarray(sweeps.transpose(2, 0, 3, 1).reshape(C, 4, TAPS * C)),
    }
    nc = _bacc.Bacc("TRN2", target_bir_lowering=False, num_devices=1)
    args = [nc.dram_tensor(name, a.shape, F32, kind="ExternalInput").ap() for name, a in arrays.items()]
    out = nc.dram_tensor("out_dram", (IMAGES, C, L), F32, kind="ExternalOutput").ap()
    build(nc, *args, out)
    r = _run(nc, [arrays], core_ids=[0])
    return r.results[0]["out_dram"].reshape(IMAGES, C, SIDE, SIDE)
```

```python
from contextlib import ExitStack

import numpy as np
import concourse.bass as bass
from concourse import mybir

F32 = mybir.dt.float32
F32R = mybir.dt.float32r
ACT = mybir.ActivationFunctionType
ALU = mybir.AluOpType
AX = mybir.AxisListType

IMAGES, C, SIDE = 104, 128, 16
L = SIDE * SIDE
T = 26
B = IMAGES // T
HEADS = 4
DH = C // HEADS
SCALE = float(DH) ** -0.5
GROUP = C // 32
TAPS = 9
STEPS = SIDE - 1
QT = L // 128
UNITS = HEADS * QT
PARTS = 3 * DH
ROWS = PARTS + 2

W_Q, W_K, W_V, W_O, AVG, IDENT, BIAS = 0, 128, 256, 384, 512, 640, 768
B_Q, B_K, B_V, B_O = BIAS, BIAS + 1, BIAS + 2, BIAS + 3
SMALL = BIAS + 4


def neighbours():
    angles = [(0, 90), (0, -90)]
    for i in range(1, 4):
        angles += [(45 * j, -90 + 45 * i) for j in range(8)]
    angles = np.array(angles)
    d = np.abs(angles.reshape(T, 1, 2) - angles.reshape(1, T, 2))
    d = np.sum(np.minimum(d, 360 - d), axis=2)
    near = d == 45
    near[0, -8::2] = True
    near[-8::2, 0] = True
    near[1, 2:10:2] = True
    near[2:10:2, 1] = True
    return [[int(j) for j in np.argwhere(near[i]).reshape(-1)] for i in range(T)]


NEAR = neighbours()


def column(j, rings=(1, 2, 3)):
    return [2 + 8 * (i - 1) + j for i in rings]


ORDER = (column(1) + column(2, (2, 1, 3)) + column(0) + column(3) + column(7) + [0, 1]
         + column(4) + column(6, (1, 3, 2)) + column(5))
PREP = (column(1) + column(2, (2,)) + column(0, (2,)) + column(2, (1, 3)) + column(0, (1, 3)) + column(3)
        + [0, 1] + column(7) + column(4) + column(6) + column(5))
LEAD = 14
KEYS = [NEAR[m] for m in ORDER]
UNIT0 = [2 * sum(len(n) for n in KEYS[:p]) for p in range(T + 1)]
ALL_UNITS = UNIT0[T]
PAIRS = ALL_UNITS // 2
NEEDS = [max(PREP.index(m) for m in KEYS[p]) for p in range(T)]
LAST_USE = [max(p for p in range(T) if m in KEYS[p]) for m in range(T)]
assert sorted(ORDER) == sorted(PREP) == list(range(T))
for _j, _m in enumerate(PREP):
    assert LAST_USE[_m] < T + _j - LEAD
    assert _j - LEAD + 2 <= min(_p for _p in range(T) if _m in KEYS[_p]) - 2

PLACE = (list(range(4)) * T)[:20] + [0, 1, 2, 0, 1, 2]
PLACE_USES = [PLACE.count(k) for k in range(4)]
P_RING, S_RING = 4, 2
TILE = 4


def place_before(p):
    return max(q for q in range(-T, p) if PLACE[q % T] == PLACE[p])


def live(b, t):
    return not isinstance(b, int) or 0 <= b * T + t < IMAGES


def prepared(b, i):
    b, j = (b + 1, i - (T - LEAD)) if i >= T - LEAD else (b, i + LEAD)
    return (b, j) if not isinstance(b, int) or 0 <= b < B else None


def need(engine, semaphore, b, per_sample, count):
    if not isinstance(b, int):
        engine.wait_ge(semaphore, b * per_sample + count)
    elif b * per_sample + count > 0:
        engine.wait_ge(semaphore, b * per_sample + count)


def walk(engine, body):
    body(-1, range(8 * (T - LEAD - 1), 8 * T))
    body(0, range(8 * T))
    with engine.Fori(1, B - 1) as b:
        body(b, range(8 * T))
    body(B - 1, range(8 * T))
    body(B, range(20))


def build(nc, x, small, w_sweep, out):
    y_dram = nc.dram_tensor("y_after_attention", (IMAGES, C, L), F32, kind="Internal").ap()
    parts_dram = nc.dram_tensor("parts_of_k_and_q", (T, 4, C, L), F32, kind="Internal").ap()
    x_b = x.rearrange("(b t) c l -> b t c l", t=T)
    y_b = y_dram.rearrange("(b t) c l -> b t c l", t=T)
    x_all = x.rearrange("i c l -> c i l")
    y_all = y_dram.rearrange("i c l -> c i l")
    out_all = out.rearrange("i c l -> c i l")

    ctx = ExitStack()
    attention = ExitStack()
    with ctx:
        def sem(name):
            return ctx.enter_context(nc.semaphore(name))

        def sb(stack, name, shape, dt=F32):
            return stack.enter_context(nc.sbuf_tensor(name, shape, dt))

        cst = sb(ctx, "cst", [128, SMALL])
        stats = sb(ctx, "stats", [128, IMAGES, 6])
        work = sb(ctx, "work", [128, 5, IMAGES])
        norm = sb(ctx, "norm", [128, 2, IMAGES])
        out_bias = sb(ctx, "out_bias", [128, 1])
        ones = sb(ctx, "ones", [128, DH])

        kstack = sb(attention, "kstack", [128, T, HEADS, L], F32R)
        v = sb(attention, "v", [128, T, QT * C])
        probs = sb(attention, "probs", [128, P_RING, HEADS * L])
        sums = sb(attention, "sums", [128, S_RING, HEADS * L])
        qstack = sb(attention, "qstack", [128, 4, HEADS, L], F32R)
        x_k = sb(attention, "x_k", [128, 2, L])
        g = sb(attention, "g", [128, 2, L])
        parts = sb(attention, "parts", [128, 2, 4, L], F32R)
        x_t = sb(attention, "x_t", [128, 2, L])
        row_max = sb(attention, "row_max", [128, 2, UNITS, 2])
        neg_max = sb(attention, "neg_max", [128, UNITS])
        max_parts = sb(attention, "max_parts", [128, 2, 2 * UNITS], F32R)
        max_rows = sb(attention, "max_rows", [2 * UNITS, 2, 128], F32R)
        recip = sb(attention, "recip", [128, L])
        attn = sb(attention, "attn", [128, 2, L])
        y_t = sb(attention, "y_t", [128, 2, L])
        norm_b = sb(attention, "norm_b", [128, 2, T])
        attention.close()

        PI = 2 * T
        xs = [sb(ctx, f"xs{p}", [128, PI, SIDE, SIDE]) for p in range(2)]
        w_raw = sb(ctx, "w_raw", [128, 2, TAPS * C])
        w_hi = sb(ctx, "w_hi", [128, 4, TAPS * C], F32R)
        w_lo = sb(ctx, "w_lo", [128, 4, TAPS * C], F32R)
        row_hi = sb(ctx, "row_hi", [128, 2, SIDE * T], F32R)
        row_lo = sb(ctx, "row_lo", [128, 2, SIDE * T], F32R)
        y_back = sb(ctx, "y_back", [128, 2, 4 * L])

        ps_t = [ctx.enter_context(nc.psum_tensor(f"ps_t{i}", [128, 512], F32)) for i in range(3)]
        ps_m = [ctx.enter_context(nc.psum_tensor(f"ps_m{i}", [128, 512], F32)) for i in range(2)]
        ps_o = [ctx.enter_context(nc.psum_tensor(f"ps_o{i}", [128, 512], F32)) for i in range(2)]
        ps_x = ctx.enter_context(nc.psum_tensor("ps_x", [128, 512], F32))

        s_small = sem("small_loaded")
        s_const = sem("constants_set")
        s_pre = [sem(f"statistics_x_loaded{i}") for i in range(P_RING)]
        s_read = sem("statistics_x_read")
        s_link = sem("dve_step")
        s_mean = sem("channel_means_made")
        s_var = sem("channel_variances_made")
        s_veps = sem("group_variance_plus_eps_made")
        s_ob = sem("value_bias_projected")
        s_ob2 = sem("output_bias_made")
        s_avg = sem("group_average_made")
        s_rt = sem("square_root_made")
        s_norm = sem("norm_tables_made")
        s_normb = sem("norm_of_sample_ready")
        s_xk = [sem(f"x_to_prepare_loaded{i}") for i in range(2)]
        s_g = sem("g_made")
        s_kq = sem("k_and_q_projected")
        s_hi_p = sem("hi_parts_made")
        s_klo = sem("k_lo_made")
        s_qlo = sem("q_lo_made")
        s_vp = sem("v_projected")
        s_v = sem("v_copied")
        s_wr = [sem(f"parts_written{i}") for i in range(2)]
        s_ks = [sem(f"keys_stacked{i}") for i in range(2)]
        s_xt = [sem(f"x_to_add_loaded{i}") for i in range(2)]
        s_qs = [sem(f"query_stacked{i}") for i in range(4)]
        s_ms = [sem(f"row_scores_made{i}") for i in range(2)]
        s_mr = [sem(f"row_max_made{i}") for i in range(2)]
        s_neg = sem("negative_max_made")
        s_mhi = sem("max_hi_made")
        s_mp = sem("max_parts_made")
        s_mt = sem("max_transposed")
        s_mc = sem("max_rows_copied")
        s_mk = [sem(f"max_stacked{i}") for i in range(2)]
        s_t = sem("scores_made")
        s_e = sem("exp_made")
        s_pv = sem("values_product_made")
        s_ps = sem("pair_summed")
        s_d = sem("row_sums_made")
        s_rc = sem("row_sums_inverted")
        s_n = sem("attention_divided")
        s_op = sem("output_projected")
        s_y = sem("y_made")
        s_st = sem("y_stats_made")
        s_ys = [sem(f"y_stored{i}") for i in range(2)]
        s_w = [sem(f"sweep_w_loaded{i}") for i in range(2)]
        s_whi = sem("sweep_w_hi_made")
        s_wsp = sem("sweep_w_split")
        s_yl = [sem(f"first_pair_y_loaded{i}") for i in range(2 * T // 4)]
        s_yl2 = sem("second_pair_y_loaded")
        s_xn = [sem(f"pair_normalised{i}") for i in range(2)]
        s_cv = [sem(f"conv_made{i}") for i in range(2)]
        s_new = [sem(f"new_row_made{i}") for i in range(2)]
        s_hi = [sem(f"row_hi_made{i}") for i in range(2)]
        s_lo = [sem(f"row_lo_made{i}") for i in range(2)]
        s_yb = [sem(f"y_reloaded{i}") for i in range(2)]
        s_yp = sem("pair_b_y_reloaded")
        s_fa = sem("first_pair_added")
        s_fb = sem("second_pair_added")
        s_out = sem("out_stored")

        HALF = T // 2
        FIRST_TILES = -(-T // TILE)
        TILES = IMAGES // TILE
        PG = PI // 4
        FINAL_SPLITS = 62
        FILL = 8 * (T - LEAD)

        def fill_tiles(b, s):
            if not isinstance(b, int) or b != -1 or s < FILL:
                return range(0)
            at = FIRST_TILES + 2 * (s - FILL) // 8
            return range(at, at + 1) if (s - FILL) % 4 == 0 and at < TILES else range(0)

        def filled(b, s):
            return isinstance(b, int) and b == -1 and s == 8 * T - 1

        block = ctx.enter_context(nc.Block())

        FIRST, REST, ALL = slice(0, T), slice(T, IMAGES), slice(0, IMAGES)

        def scores_until(p):
            return UNIT0[p % T + 1] + p // T * ALL_UNITS

        def store(queue, pair, k, added):
            queue.wait_ge(added, k + 1)
            queue.dma_start(out_all[:, pair * PI + 4 * k:pair * PI + 4 * k + 4, :],
                            xs[pair][:, 4 * k:4 * k + 4, :, :].rearrange("c i h w -> c i (h w)")
                            ).then_inc(s_out, 16)

        def parts_of(row, c):
            return row[:, c, :].rearrange("c (p i) -> c p i", i=T)

        def place(d, j):
            return j if d % 2 == 0 else j * -1 + STEPS

        def line(xp, c, d, at):
            one = xp[:, c * T:c * T + T, bass.ds(at, 1), :] if d < 2 else xp[:, c * T:c * T + T, :, bass.ds(at, 1)]
            return one.rearrange("c i a w -> c (a w) i") if d < 2 else one.rearrange("c i h a -> c (h a) i")

        @block.sync
        def _(sp):
            sp.dma_start(cst[:, :], small).then_inc(s_small, 16)

            def load_tile(n):
                if n >= P_RING:
                    sp.wait_ge(s_read, n - P_RING + 1)
                sp.dma_start(probs[:, n % P_RING, :].rearrange("c (i l) -> c i l", l=L),
                             x_all[:, TILE * n:TILE * n + TILE, :]).then_inc(s_pre[n % P_RING], 16)

            for n in range(FIRST_TILES):
                load_tile(n)

            def body(b, slots):
                for s in slots:
                    i, r = divmod(s, 8)
                    for n in fill_tiles(b, s):
                        load_tile(n)
                    if r == 0:
                        nxt = prepared(b, i + 1) if i + 1 < T else prepared(b + 1, 0)
                        if nxt:
                            bp, j = nxt
                            sp.dma_start(x_k[:, j % 2, :], x_b[bp][PREP[j], :, :]).then_inc(s_xk[j % 2], 16)
                        if live(b, i - 1):
                            db, p = divmod(i - 1, T)
                            if not prepared(b, i - 1):
                                need(sp, s_y, b + db, T, p - 1)
                            sp.dma_start(x_t[:, p % 2, :], x_b[b + db][ORDER[p], :, :]).then_inc(s_xt[p % 2], 16)
                    if r == 4 and prepared(b, i):
                        bp, j = prepared(b, i)
                        need(sp, s_qlo, bp, T, j + 1)
                        sp.dma_start(parts_dram[PREP[j]].rearrange("k c l -> c k l"),
                                     parts[:, j % 2, :, :].bitcast(F32)).then_inc(s_wr[j % 2], 16)
                    before = prepared(b, i - 1)
                    if r == 5 and before:
                        bp, j = before
                        m = PREP[j]
                        need(sp, s_wr[j % 2], bp, 16 * HALF, 16 * (j // 2 + 1))
                        if not prepared(b, i):
                            need(sp, s_ks[j % 2], bp, 48 * HALF, 48 * (j // 2))
                        for row, part in enumerate((0, 1, 0)):
                            sp.dma_start(kstack[DH * row:DH * row + DH, m, :, :].bitcast(F32),
                                         parts_dram[m, part].rearrange("(h d) l -> d h l", d=DH)
                                         ).then_inc(s_ks[j % 2], 16)
                    if r == 7 and live(b, i + 3):
                        db, p = divmod(i + 3, T)
                        need(sp, s_t, b + db, 2 * ALL_UNITS, 2 * scores_until(place_before(p)))
                        for row, part in enumerate((2, 2, 3)):
                            sp.dma_start(qstack[DH * row:DH * row + DH, PLACE[p], :, :].bitcast(F32),
                                         parts_dram[ORDER[p], part].rearrange("(h d) l -> d h l", d=DH)
                                         ).then_inc(s_qs[PLACE[p]], 16)

            walk(sp, body)

            sp.wait_ge(s_st, IMAGES)
            for i in range(2):
                sp.wait_ge(s_ys[i], 16 * B * HALF)
            for d in range(2):
                sp.dma_start(w_raw[:, d, :], w_sweep[:, d, :]).then_inc(s_w[d], 16)
            for k in range(PG):
                sp.dma_start(xs[0][:, 4 * k:4 * k + 4, :, :].rearrange("c i h w -> c i (h w)"),
                             y_all[:, 4 * k:4 * k + 4, :]).then_inc(s_yl[k], 16)
            for d in range(2, 4):
                sp.wait_ge(s_wsp, d - 1)
                sp.dma_start(w_raw[:, d - 2, :], w_sweep[:, d, :]).then_inc(s_w[d - 2], 16)
            for k in range(PG):
                sp.dma_start(xs[1][:, 4 * k:4 * k + 4, :, :].rearrange("c i h w -> c i (h w)"),
                             y_all[:, PI + 4 * k:PI + 4 * k + 4, :]).then_inc(s_yl2, 16)
            for k in range(PG):
                if k >= 2:
                    sp.wait_ge(s_fa, k - 1)
                sp.dma_start(y_back[:, k % 2, :].rearrange("c (i l) -> c i l", l=L),
                             y_all[:, 4 * k:4 * k + 4, :]).then_inc(s_yb[k % 2], 16)
                if k >= 1:
                    store(sp, 0, k - 1, s_fa)
            store(sp, 0, PG - 1, s_fa)
            sp.wait_ge(s_out, 16 * PG)
            sp.dma_start(xs[0][:, :, :, :].rearrange("c i h w -> c i (h w)"),
                         y_all[:, PI:2 * PI, :]).then_inc(s_yp, 16)
            for k in range(PG):
                store(sp, 1, k, s_fb)
            sp.wait_ge(s_out, 16 * 2 * PG)

        @block.gpsimd
        def _(pool):
            pool.memset(ones[:, :], 1.0).then_inc(s_const, 1)
            pool.wait_ge(s_const, 1)
            pool.memset(kstack[PARTS:ROWS, :, :, :].bitcast(F32), 1.0).then_inc(s_const, 1)

            def body(b):
                for p in range(PAIRS):
                    need(pool, s_e, b, 2 * ALL_UNITS, 4 * p + 4)
                    need(pool, s_d, b, PAIRS, p - S_RING + 1)
                    nc.gpsimd.tensor_tensor(sums[:, p % S_RING, :], probs[:, 2 * p % P_RING, :],
                                            probs[:, (2 * p + 1) % P_RING, :], ALU.add).then_inc(s_ps, 1)

            body(0)
            with pool.Fori(1, B) as b:
                body(b)
            pool.wait_ge(s_norm, 3)
            pool.wait_ge(s_yl2, 16 * PG)
            for i in range(PI):
                last = nc.gpsimd.tensor_scalar(xs[1][:, i, :, :], xs[1][:, i, :, :],
                                               norm[:, 0, PI + i:PI + i + 1], norm[:, 1, PI + i:PI + i + 1],
                                               ALU.mult, ALU.add)
            last.then_inc(s_xn[1], 1)
            for c in range(2):
                pool.wait_ge(s_lo[c], FINAL_SPLITS)
            for k in range(PG):
                pool.wait_ge(s_yb[k % 2], 16 * (k // 2 + 1))
                part = xs[0][:, 4 * k:4 * k + 4, :, :].rearrange("c i h w -> c (i h w)")
                nc.gpsimd.tensor_tensor(part, part, y_back[:, k % 2, :], ALU.add).then_inc(s_fa, 1)

        @block.scalar
        def _(act):
            def square_root(which, images):
                act.wait_ge(s_veps, which + 1)
                nc.scalar.activation(work[:, 3, images], work[:, 2, images], ACT.Sqrt).then_inc(s_rt, 1)

            square_root(0, FIRST)

            def body(b, slots):
                for s in slots:
                    i, r = divmod(s, 8)
                    if r == 2 and prepared(b, i):
                        bp, j = prepared(b, i)
                        need(act, s_kq, bp, T, j + 1)
                        need(act, s_wr[j % 2], bp, 16 * HALF, 16 * (j // 2))
                        nc.scalar.activation(parts[:, j % 2, 0, :], ps_x[:, 0:L], ACT.Identity,
                                             bias=cst[:, B_K:B_K + 1]).then_inc(s_hi_p, 1)
                        nc.scalar.activation(parts[:, j % 2, 2, :], ps_x[:, L:2 * L], ACT.Identity,
                                             bias=cst[:, B_Q:B_Q + 1]).then_inc(s_hi_p, 1)
                    if r == 4 and prepared(b, i):
                        bp, j = prepared(b, i)
                        need(act, s_vp, bp, T, j + 1)
                        need(act, s_pv, bp - 1, ALL_UNITS, UNIT0[LAST_USE[PREP[j]] + 1])
                        nc.scalar.activation(v[:, PREP[j], :], ps_x[:, 0:QT * C], ACT.Copy).then_inc(s_v, 1)
                    if r == 6 and live(b, i + 1):
                        db, p = divmod(i + 1, T)
                        need(act, s_mc, b + db, T, p + 1)
                        for part in range(2):
                            act.dma_start(
                                qstack[PARTS + part:PARTS + part + 1, PLACE[p], :, :].bitcast(F32)
                                .rearrange("p h (k l) -> p (h k) l", l=128),
                                max_rows[UNITS * part:UNITS * part + UNITS, p % 2, :].bitcast(F32)
                            ).then_inc(s_mk[p % 2], 16)
                    if live(b, i) and i < T and r < 2 * len(KEYS[i]):
                        n = UNIT0[i] + r
                        for half in range(2):
                            need(act, s_t, b, 2 * ALL_UNITS, 2 * n + half + 1)
                            if half == 0:
                                need(act, s_pv, b, ALL_UNITS, n - P_RING + 1)
                                need(act, s_ps, b, PAIRS, (n - P_RING) // 2 + 1)
                            nc.scalar.activation(probs[:, n % P_RING, 512 * half:512 * half + 512],
                                                 ps_t[(2 * n + half) % 3][:, :], ACT.Exp,
                                                 scale=SCALE).then_inc(s_e, 1)
                    if r == 2 and live(b, i - 2):
                        db, p = divmod(i - 2, T)
                        need(act, s_y, b + db, T, p + 1)
                        act.dma_start(y_b[b + db][ORDER[p], :, :], y_t[:, p % 2, :]).then_inc(s_ys[p % 2], 16)
                    if filled(b, s):
                        square_root(1, REST)

            walk(act, body)
            square_root(2, ALL)

            for pair in range(2):
                done, splits = 4 * STEPS * pair, FINAL_SPLITS * pair
                for d in range(4):
                    if d % 2 == 0:
                        if d == 0:
                            act.wait_ge(s_xn[pair], 1)
                        for c in range(2):
                            if splits:
                                act.wait_ge(s_lo[c], splits)
                            nc.scalar.activation(parts_of(row_hi, c), line(xs[pair], c, d, 0),
                                                 ACT.Copy).then_inc(s_hi[c], 1)
                        splits += 1
                    with act.Fori(1, STEPS + 1) as j:
                        for c in range(2):
                            act.wait_ge(s_new[c], j + done)
                            nc.scalar.activation(parts_of(row_hi, c), line(xs[pair], c, d, place(d, j)),
                                                 ACT.Copy).then_inc(s_hi[c], 1)
                    done += STEPS
                    splits += STEPS

        @block.vector
        def _(dve):
            vec = nc.vector
            links = [0]

            def link(ins):
                links[0] += 1
                ins.then_inc(s_link, 1)
                dve.wait_ge(s_link, links[0])

            def norm_tables(which, images):
                mean, var, t2, root, scratch = (work[:, i, images] for i in range(5))
                stat = [stats[:, images, k] for k in range(6)]
                scale, bias = norm[:, 0, images], norm[:, 1, images]
                link(vec.tensor_tensor(t2, stat[1], stat[4], ALU.subtract))
                link(vec.tensor_scalar(scratch, t2, 0.5, None, ALU.mult))
                link(vec.tensor_tensor(t2, scratch, scratch, ALU.mult))
                link(vec.tensor_tensor(var, stat[2], stat[5], ALU.add))
                link(vec.scalar_tensor_tensor(var, var, 1.0 / L, t2, ALU.mult, ALU.add))
                link(vec.tensor_tensor(scratch, stat[1], stat[4], ALU.add))
                vec.tensor_scalar(mean, scratch, 0.5, None, ALU.mult).then_inc(s_mean, 1)
                dve.wait_ge(s_avg, 2 * which + 1)
                link(vec.tensor_tensor(t2, mean, ps_x[:, images], ALU.subtract))
                link(vec.tensor_tensor(scratch, t2, t2, ALU.mult))
                link(vec.tensor_scalar(bias, ps_x[:, images], -1.0, None, ALU.mult))
                vec.tensor_tensor(var, scratch, var, ALU.add).then_inc(s_var, 1)
                dve.wait_ge(s_avg, 2 * which + 2)
                vec.tensor_scalar(t2, ps_x[:, slice(images.start + 128, images.stop + 128)], 1e-5, None,
                                  ALU.add).then_inc(s_veps, 1)
                dve.wait_ge(s_rt, which + 1)
                link(vec.reciprocal(scale, root))
                link(vec.tensor_tensor(scratch, scale, scale, ALU.mult))
                link(vec.tensor_tensor(scratch, scratch, t2, ALU.mult))
                link(vec.tensor_scalar(scratch, scratch, -0.5, 1.5, ALU.mult, ALU.add))
                link(vec.tensor_tensor(scale, scale, scratch, ALU.mult))
                vec.tensor_tensor(bias, bias, scale, ALU.mult).then_inc(s_norm, 1)
                dve.wait_ge(s_norm, which + 1)

            def read_tile(n):
                dve.wait_ge(s_pre[n % P_RING], 16 * (n // P_RING + 1))
                for k in range(TILE):
                    last = vec.bn_stats(stats[:, TILE * n + k, :], probs[:, n % P_RING, L * k:L * k + L])
                last.then_inc(s_read, 1)

            for n in range(FIRST_TILES):
                read_tile(n)
            dve.wait_ge(s_read, FIRST_TILES)
            dve.wait_ge(s_small, 16)
            dve.wait_ge(s_ob, 1)
            vec.tensor_scalar(out_bias[:, :], ps_x[:, 256:257], cst[:, B_O:B_O + 1], None, ALU.add).then_inc(s_ob2, 1)
            norm_tables(0, FIRST)

            def body(b, slots):
                def row_maxima(p, db, w):
                    for half in range(2):
                        n = len(KEYS[p][2 * half:2 * half + 2])
                        need(dve, s_ms[half], b + db, T * UNITS, UNITS * p + w + 1)
                        vec.tensor_reduce(row_max[:, p % 2, w, half:half + 1], ps_m[half][:, 0:n * L],
                                          AX.X, ALU.max).then_inc(s_mr[half], 1)

                def invert(p, db, piece):
                    part = slice(L // 4 * piece, L // 4 * piece + L // 4)
                    if piece == 0:
                        need(dve, s_d, b + db, PAIRS, UNIT0[p + 1] // 2)
                        need(dve, s_n, b + db, T, p)
                    vec.reciprocal(recip[:, part], ps_o[p % 2][:, L + part.start:L + part.stop]).then_inc(s_rc, 1)

                for s in slots:
                    i, r = divmod(s, 8)
                    prep = prepared(b, i)
                    for n in fill_tiles(b, s - 4):
                        read_tile(n)
                    if r == 0 and live(b, i - 2):
                        db, p = divmod(i - 2, T)
                        need(dve, s_rc, b + db, 4 * T, 4 * p + 4)
                        need(dve, s_op, b + db, T, p - 1)
                        vec.tensor_tensor(attn[:, p % 2, :], ps_o[p % 2][:, 0:L], recip[:, :],
                                          ALU.mult).then_inc(s_n, 1)
                    if r == 1 and live(b, i - 2):
                        db, p = divmod(i - 2, T)
                        need(dve, s_op, b + db, T, p + 1)
                        need(dve, s_xt[p % 2], b + db, 16 * HALF, 16 * (p // 2 + 1))
                        need(dve, s_ys[p % 2], b + db, 16 * HALF, 16 * (p // 2))
                        vec.scalar_tensor_tensor(y_t[:, p % 2, :], ps_x[:, 0:L], out_bias[:, 0:1],
                                                 x_t[:, p % 2, :], ALU.add, ALU.add).then_inc(s_y, 1)
                    q, w = divmod(s + 14, 8)
                    if live(b, q):
                        db, p = divmod(q, T)
                        row_maxima(p, db, w)
                        if w == UNITS - 1:
                            for half in range(2):
                                need(dve, s_mr[half], b + db, T * UNITS, UNITS * (p + 1))
                            vec.tensor_reduce(neg_max[:, :], row_max[:, p % 2, :, :], AX.X, ALU.max,
                                              negate=True).then_inc(s_neg, 1)
                            need(dve, s_mt, b + db, T, p - 1)
                            need(dve, s_neg, b + db, T, p + 1)
                            vec.tensor_copy(max_parts[:, p % 2, 0:UNITS], neg_max[:, :]).then_inc(s_mhi, 1)
                            need(dve, s_mhi, b + db, T, p + 1)
                            vec.tensor_tensor(max_parts[:, p % 2, UNITS:2 * UNITS], neg_max[:, :],
                                              max_parts[:, p % 2, 0:UNITS].bitcast(F32),
                                              ALU.subtract).then_inc(s_mp, 1)
                    if r == 0 and prep:
                        bp, j = prep
                        m = PREP[j]
                        if j == 0:
                            vec.tensor_copy(norm_b[:, :, :], norm[:, :, bass.ds(bp * T, T)]).then_inc(s_normb, 1)
                            need(dve, s_normb, bp, 1, 1)
                        need(dve, s_xk[j % 2], bp, 16 * HALF, 16 * (j // 2 + 1))
                        need(dve, s_vp, bp, T, j - 1)
                        vec.tensor_scalar(g[:, j % 2, :], x_k[:, j % 2, :], norm_b[:, 0, m:m + 1],
                                          norm_b[:, 1, m:m + 1], ALU.mult, ALU.add).then_inc(s_g, 1)
                    if r in (2, 3) and prep:
                        bp, j = prep
                        k = r - 2
                        need(dve, s_hi_p, bp, 2 * T, 2 * j + 2)
                        bias = (B_K, B_Q)[k]
                        vec.scalar_tensor_tensor(parts[:, j % 2, 2 * k + 1, :], ps_x[:, L * k:L * k + L],
                                                 cst[:, bias:bias + 1], parts[:, j % 2, 2 * k, :].bitcast(F32),
                                                 ALU.add, ALU.subtract).then_inc((s_klo, s_qlo)[k], 1)
                    if r == 2 and live(b, i - 2):
                        db, p = divmod(i - 2, T)
                        need(dve, s_y, b + db, T, p + 1)
                        vec.bn_stats(stats[:, bass.ds((b + db) * T + ORDER[p], 1), :].rearrange("c a k -> c (a k)"),
                                     y_t[:, p % 2, :]).then_inc(s_st, 1)
                    if r >= 4 and live(b, i - 1):
                        db, p = divmod(i - 1, T)
                        invert(p, db, r - 4)
                    if r == 5 and live(b, i + 1):
                        db, p = divmod(i + 1, T)
                        need(dve, s_mt, b + db, T, p + 1)
                        need(dve, s_mk[p % 2], b + db, 32 * HALF, 32 * (p // 2))
                        vec.tensor_copy(max_rows[:, p % 2, :], ps_x[0:2 * UNITS, 0:128]).then_inc(s_mc, 1)
                    if filled(b, s):
                        dve.wait_ge(s_read, TILES)
                        norm_tables(1, REST)

            walk(dve, body)

            dve.wait_ge(s_st, IMAGES)
            norm_tables(2, ALL)
            for i in range(2):
                dve.wait_ge(s_ys[i], 16 * B * HALF)

            def split_weights(d):
                dve.wait_ge(s_w[d % 2], 16 * (d // 2 + 1))
                vec.tensor_copy(w_hi[:, d, :], w_raw[:, d % 2, :]).then_inc(s_whi, 1)
                dve.wait_ge(s_whi, d + 1)
                vec.tensor_tensor(w_lo[:, d, :], w_raw[:, d % 2, :], w_hi[:, d, :].bitcast(F32),
                                  ALU.subtract).then_inc(s_wsp, 1)

            split_weights(0)
            split_weights(1)
            for k in range(PG):
                dve.wait_ge(s_yl[k], 16)
                for i in range(4 * k, 4 * k + 4):
                    last = vec.tensor_scalar(xs[0][:, i, :, :], xs[0][:, i, :, :],
                                             norm[:, 0, i:i + 1], norm[:, 1, i:i + 1], ALU.mult, ALU.add)
            last.then_inc(s_xn[0], 1)
            for pair in range(2):
                done, splits = 4 * STEPS * pair, FINAL_SPLITS * pair

                def row_parts(c, d, at, count):
                    dve.wait_ge(s_hi[c], count)
                    vec.tensor_tensor(parts_of(row_lo, c), line(xs[pair], c, d, at),
                                      parts_of(row_hi, c).bitcast(F32), ALU.subtract).then_inc(s_lo[c], 1)

                for d in range(4):
                    if d % 2 == 0:
                        splits += 1
                        for c in range(2):
                            row_parts(c, d, 0, splits)
                    with dve.Fori(1, STEPS + 1) as j:
                        at = dve.snap(place(d, j))
                        for c in range(2):
                            dve.wait_ge(s_cv[c], j + done)
                            now = line(xs[pair], c, d, at)
                            vec.scalar_tensor_tensor(now, ps_t[c][:, 0:SIDE * T].rearrange("c (p i) -> c p i", i=T),
                                                     0.0, now, ALU.max, ALU.add).then_inc(s_new[c], 1)
                            row_parts(c, d, at, j + splits)
                    if pair == 0 and d == 0:
                        split_weights(2)
                        split_weights(3)
                    done += STEPS
                    splits += STEPS
            for c in range(2):
                dve.wait_ge(s_lo[c], 2 * FINAL_SPLITS)
            dve.wait_ge(s_yp, 16)
            for k in range(PG):
                part = xs[1][:, 4 * k:4 * k + 4, :, :].rearrange("c i h w -> c (i h w)")
                back = xs[0][:, 4 * k:4 * k + 4, :, :].rearrange("c i h w -> c (i h w)")
                vec.tensor_tensor(part, part, back, ALU.add).then_inc(s_fb, 1)

        @block.tensor
        def _(pe):
            mm = nc.tensor.matmul

            def group_averages(which, images):
                pe.wait_ge(s_mean, which + 1)
                mm(ps_x[:, images], cst[:, AVG:AVG + 128], work[:, 0, images], start=True, stop=True).then_inc(s_avg, 1)
                pe.wait_ge(s_var, which + 1)
                mm(ps_x[:, slice(images.start + 128, images.stop + 128)], cst[:, AVG:AVG + 128],
                   work[:, 1, images], start=True, stop=True).then_inc(s_avg, 1)

            pe.wait_ge(s_small, 16)
            mm(ps_x[:, 256:257], cst[:, W_O:W_O + 128], cst[:, B_V:B_V + 1], start=True, stop=True).then_inc(s_ob, 1)
            pe.wait_ge(s_ob2, 1)
            group_averages(0, FIRST)
            pe.wait_ge(s_const, 2)

            def body(b, slots):
                for s in slots:
                    i, r = divmod(s, 8)
                    prep = prepared(b, i)
                    if r == 5 and live(b, i + 1):
                        db, p = divmod(i + 1, T)
                        bank_of_v_copied(b, i)
                        need(pe, s_mp, b + db, T, p + 1)
                        mm(ps_x[0:2 * UNITS, 0:128], max_parts[:, p % 2, :].bitcast(F32),
                           cst[:, IDENT:IDENT + 128], start=True, stop=True).then_inc(s_mt, 1)
                    q, w = divmod(s + 14, 8)
                    if live(b, q):
                        db, p = divmod(q, T)
                        h, qt = divmod(w, QT)
                        if w == 0:
                            for k in range(2):
                                need(pe, s_ks[k], b + db, 48 * HALF, 48 * ((NEEDS[p] - k) // 2 + 1))
                            need(pe, s_qs[PLACE[p]], b + db, 48 * PLACE_USES[PLACE[p]],
                                 48 * PLACE[:p + 1].count(PLACE[p]))
                        for half in range(2):
                            need(pe, s_mr[half], b + db, T * UNITS, UNITS * p + w)
                            for k, m in enumerate(KEYS[p][2 * half:2 * half + 2]):
                                last = mm(ps_m[half][:, L * k:L * k + L],
                                          qstack[0:PARTS, PLACE[p], h, 128 * qt:128 * qt + 128],
                                          kstack[0:PARTS, m, h, :], start=True, stop=True)
                            last.then_inc(s_ms[half], 1)
                    if live(b, i) and i < T and r < 2 * len(KEYS[i]):
                        n = UNIT0[i] + r
                        m, kt = KEYS[i][r // 2], r % 2
                        if r == 0:
                            need(pe, s_mk[i % 2], b, 32 * HALF, 32 * (i // 2 + 1))
                        for half in range(2):
                            need(pe, s_e, b, 2 * ALL_UNITS, 2 * n + half - 2)
                            for k in range(2):
                                last = mm(ps_t[(2 * n + half) % 3][:, L * k:L * k + L],
                                          kstack[0:ROWS, m, 2 * half + k, 128 * kt:128 * kt + 128],
                                          qstack[0:ROWS, PLACE[i], 2 * half + k, :], start=True, stop=True)
                            last.then_inc(s_t, 1)
                    q, u = divmod(s - 1, 8)
                    if live(b, q) and q < T and u < 2 * len(KEYS[q % T]):
                        db, p = divmod(q, T)
                        n = UNIT0[p] + u
                        m, kt = KEYS[p][u // 2], u % 2
                        if u == 0:
                            need(pe, s_n, b + db, T, p - 1)
                            need(pe, s_v, b + db, T, NEEDS[p] + 1)
                        need(pe, s_e, b + db, 2 * ALL_UNITS, 2 * n + 2)
                        for h in range(HEADS):
                            last = mm(ps_o[p % 2][DH * h:DH * h + DH, 0:L],
                                      v[:, m, C * kt + DH * h:C * kt + DH * h + DH],
                                      probs[:, n % P_RING, L * h:L * h + L],
                                      start=(u == 0), stop=(u == 2 * len(KEYS[p]) - 1), skip_group_check=True)
                        last.then_inc(s_pv, 1)
                    q, u = divmod(s - 4, 8)
                    if u % 2 == 0 and live(b, q) and u // 2 < len(KEYS[q % T]):
                        db, p = divmod(q, T)
                        n = UNIT0[p] // 2 + u // 2
                        need(pe, s_ps, b + db, PAIRS, n + 1)
                        for h in range(HEADS):
                            last = mm(ps_o[p % 2][DH * h:DH * h + DH, L:2 * L], ones[:, :],
                                      sums[:, n % S_RING, L * h:L * h + L],
                                      start=False, stop=(u // 2 == len(KEYS[p]) - 1), skip_group_check=True)
                        last.then_inc(s_d, 1)
                    if r == 0 and live(b, i - 2):
                        db, p = divmod(i - 2, T)
                        if live(b, i):
                            need(pe, s_mc, b, T, i + 1)
                        need(pe, s_n, b + db, T, p + 1)
                        mm(ps_x[:, 0:L], cst[:, W_O:W_O + 128], attn[:, p % 2, :], start=True, stop=True).then_inc(s_op, 1)
                    if r == 1 and prep:
                        bp, j = prep
                        if live(b, i - 2):
                            need(pe, s_y, b, T, i - 1)
                        elif live(b, i):
                            need(pe, s_mc, b, T, i + 1)
                        else:
                            need(pe, s_v, bp, T, j)
                        need(pe, s_ks[(j - 1) % 2], bp, 48 * HALF, 48 * ((j - 1) // 2))
                        need(pe, s_g, bp, T, j + 1)
                        mm(ps_x[:, 0:L], cst[:, W_K:W_K + 128], g[:, j % 2, :], start=True, stop=True)
                        mm(ps_x[:, L:2 * L], cst[:, W_Q:W_Q + 128], g[:, j % 2, :],
                           start=True, stop=True).then_inc(s_kq, 1)
                    if r == 3 and prep:
                        bp, j = prep
                        need(pe, s_klo, bp, T, j + 1)
                        need(pe, s_qlo, bp, T, j + 1)
                        for kt in range(QT):
                            last = mm(ps_x[:, C * kt:C * kt + C], g[:, j % 2, 128 * kt:128 * kt + 128],
                                      cst[:, W_V:W_V + 128], start=True, stop=True)
                        last.then_inc(s_vp, 1)
                    if filled(b, s):
                        pe.wait_ge(s_mc, 1)
                        group_averages(1, REST)

            def bank_of_v_copied(b, i):
                if prepared(b, i):
                    bp, j = prepared(b, i)
                    need(pe, s_v, bp, T, j + 1)
                else:
                    need(pe, s_y, b, T, i - 1)

            walk(pe, body)

            group_averages(2, ALL)
            for pair in range(2):
                done, splits = 0, FINAL_SPLITS * pair
                for d in range(4):
                    if pair == 0:
                        pe.wait_ge(s_wsp, d + 1)
                    if d % 2 == 0:
                        splits += 1
                    with pe.Fori(0, STEPS) as j:
                        for c in range(2):
                            pe.wait_ge(s_lo[c], j + splits)
                            taps = sorted(range(TAPS), key=lambda k: abs(k - TAPS // 2))
                            for k in taps:
                                shift = k - TAPS // 2
                                lo, hi = max(0, -shift) * T, (SIDE - max(0, shift)) * T
                                for w, row in ((w_hi, row_hi), (w_lo, row_hi), (w_hi, row_lo)):
                                    last = mm(ps_t[c][:, lo:hi], w[:, d, C * k:C * k + C],
                                              row[:, c, lo + shift * T:hi + shift * T],
                                              start=(k == taps[0] and w is w_hi and row is row_hi),
                                              stop=(k == taps[-1] and row is row_lo))
                            last.then_inc(s_cv[c], 1)
                    splits += STEPS


def kernel(x, L0_conv_w_in, L0_conv_b_in, L0_conv_w_out, L0_conv_b_out,
           L1_conv_w_down, L1_conv_w_up, L1_conv_w_right, L1_conv_w_left):
    import concourse.bacc as _bacc
    from concourse.bass_utils import run_bass_kernel_spmd as _run

    w_in = np.asarray(L0_conv_w_in)
    average = np.kron(np.eye(C // GROUP, dtype=np.float32), np.full((GROUP, GROUP), 1.0 / GROUP, np.float32))
    small = np.concatenate(
        [w_in[C * i:C * i + C].T for i in range(3)]
        + [np.asarray(L0_conv_w_out).T, average, np.eye(128, dtype=np.float32),
           np.asarray(L0_conv_b_in).reshape(3, C).T, np.asarray(L0_conv_b_out).reshape(C, 1)], axis=1)
    sweeps = np.stack([np.asarray(w) for w in (L1_conv_w_down, L1_conv_w_up, L1_conv_w_right, L1_conv_w_left)])
    arrays = {
        "x_dram": np.ascontiguousarray(np.asarray(x).reshape(IMAGES, C, L)),
        "small_dram": np.ascontiguousarray(small),
        "sweep_dram": np.ascontiguousarray(sweeps.transpose(2, 0, 3, 1).reshape(C, 4, TAPS * C)),
    }
    nc = _bacc.Bacc("TRN2", target_bir_lowering=False, num_devices=1)
    args = [nc.dram_tensor(name, a.shape, F32, kind="ExternalInput").ap() for name, a in arrays.items()]
    out = nc.dram_tensor("out_dram", (IMAGES, C, L), F32, kind="ExternalOutput").ap()
    build(nc, *args, out)
    r = _run(nc, [arrays], core_ids=[0])
    return r.results[0]["out_dram"].reshape(IMAGES, C, SIDE, SIDE)
```

```python
from contextlib import ExitStack

import numpy as np
import concourse.bass as bass
from concourse import mybir

F32 = mybir.dt.float32
F32R = mybir.dt.float32r
ACT = mybir.ActivationFunctionType
ALU = mybir.AluOpType
AX = mybir.AxisListType

IMAGES, C, SIDE = 104, 128, 16
L = SIDE * SIDE
T = 26
B = IMAGES // T
HEADS = 4
DH = C // HEADS
SCALE = float(DH) ** -0.5
GROUP = C // 32
TAPS = 9
STEPS = SIDE - 1
QT = L // 128
UNITS = HEADS * QT
PARTS = 3 * DH
ROWS = PARTS + 2

W_Q, W_K, W_V, W_O, AVG, IDENT, BIAS = 0, 128, 256, 384, 512, 640, 768
B_Q, B_K, B_V, B_O = BIAS, BIAS + 1, BIAS + 2, BIAS + 3
SMALL = BIAS + 4


def neighbours():
    angles = [(0, 90), (0, -90)]
    for i in range(1, 4):
        angles += [(45 * j, -90 + 45 * i) for j in range(8)]
    angles = np.array(angles)
    d = np.abs(angles.reshape(T, 1, 2) - angles.reshape(1, T, 2))
    d = np.sum(np.minimum(d, 360 - d), axis=2)
    near = d == 45
    near[0, -8::2] = True
    near[-8::2, 0] = True
    near[1, 2:10:2] = True
    near[2:10:2, 1] = True
    return [[int(j) for j in np.argwhere(near[i]).reshape(-1)] for i in range(T)]


NEAR = neighbours()


def column(j, rings=(1, 2, 3)):
    return [2 + 8 * (i - 1) + j for i in rings]


ORDER = (column(1) + column(2, (2, 1, 3)) + column(0) + column(3) + column(7) + [0, 1]
         + column(4) + column(6, (1, 3, 2)) + column(5))
PREP = (column(1) + column(2, (2,)) + column(0, (2,)) + column(2, (1, 3)) + column(0, (1, 3)) + column(3)
        + [0, 1] + column(7) + column(4) + column(6) + column(5))
LEAD = 14
KEYS = [NEAR[m] for m in ORDER]
UNIT0 = [2 * sum(len(n) for n in KEYS[:p]) for p in range(T + 1)]
ALL_UNITS = UNIT0[T]
assert all(len(n) in (3, 4) for n in KEYS)
SUM0 = [sum(len(n) - 1 for n in KEYS[:p]) for p in range(T + 1)]
ALL_SUMS = SUM0[T]
ADD0 = [SUM0[p] + 2 * p for p in range(T + 1)]
ALL_ADDS = ADD0[T]
ADDED = [ADD0[p] + (1, 1, 2, 3, 4, 4, 5, 5)[u] for p in range(T) for u in range(2 * len(KEYS[p]))]
NEEDS = [max(PREP.index(m) for m in KEYS[p]) for p in range(T)]
LAST_USE = [max(p for p in range(T) if m in KEYS[p]) for m in range(T)]
assert sorted(ORDER) == sorted(PREP) == list(range(T))
for _j, _m in enumerate(PREP):
    assert LAST_USE[_m] < T + _j - LEAD
    assert _j - LEAD + 2 <= min(_p for _p in range(T) if _m in KEYS[_p]) - 2

PLACE = (list(range(4)) * T)[:20] + [0, 1, 2, 0, 1, 2]
PLACE_USES = [PLACE.count(k) for k in range(4)]
P_RING, S_RING = 6, 2
assert ALL_UNITS % P_RING == 0 and ALL_SUMS % S_RING == 0
TILE = 4


def place_before(p):
    return max(q for q in range(-T, p) if PLACE[q % T] == PLACE[p])


def live(b, t):
    return not isinstance(b, int) or 0 <= b * T + t < IMAGES


def prepared(b, i):
    b, j = (b + 1, i - (T - LEAD)) if i >= T - LEAD else (b, i + LEAD)
    return (b, j) if not isinstance(b, int) or 0 <= b < B else None


def tiles_added(n):
    return ADDED[n % ALL_UNITS] + n // ALL_UNITS * ALL_ADDS


def need(engine, semaphore, b, per_sample, count):
    if not isinstance(b, int):
        engine.wait_ge(semaphore, b * per_sample + count)
    elif b * per_sample + count > 0:
        engine.wait_ge(semaphore, b * per_sample + count)


def walk(engine, body):
    body(-1, range(8 * (T - LEAD - 1), 8 * T))
    body(0, range(8 * T))
    with engine.Fori(1, B - 1) as b:
        body(b, range(8 * T))
    body(B - 1, range(8 * T))
    body(B, range(20))


def build(nc, x, small, w_sweep, out):
    y_dram = nc.dram_tensor("y_after_attention", (IMAGES, C, L), F32, kind="Internal").ap()
    parts_dram = nc.dram_tensor("parts_of_k_and_q", (T, 4, C, L), F32, kind="Internal").ap()
    x_b = x.rearrange("(b t) c l -> b t c l", t=T)
    y_b = y_dram.rearrange("(b t) c l -> b t c l", t=T)
    x_all = x.rearrange("i c l -> c i l")
    y_all = y_dram.rearrange("i c l -> c i l")
    out_all = out.rearrange("i c l -> c i l")

    ctx = ExitStack()
    attention = ExitStack()
    with ctx:
        def sem(name):
            return ctx.enter_context(nc.semaphore(name))

        def sb(stack, name, shape, dt=F32):
            return stack.enter_context(nc.sbuf_tensor(name, shape, dt))

        cst = sb(ctx, "cst", [128, SMALL])
        stats = sb(ctx, "stats", [128, IMAGES, 6])
        work = sb(ctx, "work", [128, 5, IMAGES])
        norm = sb(ctx, "norm", [128, 2, IMAGES])
        out_bias = sb(ctx, "out_bias", [128, 1])
        ones = sb(ctx, "ones", [128, DH])
        unit = sb(ctx, "unit", [128, 128], F32R)

        kstack = sb(attention, "kstack", [128, T, HEADS, L], F32R)
        v = sb(attention, "v", [128, T, QT * C])
        probs = sb(attention, "probs", [128, P_RING, HEADS * L])
        sums = sb(attention, "sums", [128, S_RING, HEADS * L])
        qstack = sb(attention, "qstack", [128, 4, HEADS, L], F32R)
        x_k = sb(attention, "x_k", [128, 2, L])
        g = sb(attention, "g", [128, 2, L])
        kq = sb(attention, "kq", [128, 2, L])
        parts = sb(attention, "parts", [128, 4, L], F32R)
        x_t = sb(attention, "x_t", [128, 2, L])
        row_max = sb(attention, "row_max", [128, 2, UNITS, 2])
        neg_max = sb(attention, "neg_max", [128, UNITS])
        max_parts = sb(attention, "max_parts", [128, 2, 2 * UNITS], F32R)
        max_rows = sb(attention, "max_rows", [2 * UNITS, 2, 128], F32R)
        recip = sb(attention, "recip", [128, L])
        attn = sb(attention, "attn", [128, 2, L])
        y_t = sb(attention, "y_t", [128, 2, L])
        norm_b = sb(attention, "norm_b", [128, 2, T])
        attention.close()

        PI = 2 * T
        xs = [sb(ctx, f"xs{p}", [128, PI, SIDE, SIDE]) for p in range(2)]
        w_raw = sb(ctx, "w_raw", [128, 2, TAPS * C])
        w_hi = sb(ctx, "w_hi", [128, 4, TAPS * C], F32R)
        w_lo = sb(ctx, "w_lo", [128, 4, TAPS * C], F32R)
        row_hi = sb(ctx, "row_hi", [128, 2, SIDE * T], F32R)
        row_lo = sb(ctx, "row_lo", [128, 2, SIDE * T], F32R)
        y_back = sb(ctx, "y_back", [128, 2, 4 * L])

        ps_t = [ctx.enter_context(nc.psum_tensor(f"ps_t{i}", [128, 512], F32)) for i in range(3)]
        ps_m = [ctx.enter_context(nc.psum_tensor(f"ps_m{i}", [128, 512], F32)) for i in range(2)]
        ps_o = [ctx.enter_context(nc.psum_tensor(f"ps_o{i}", [128, 512], F32)) for i in range(2)]
        ps_x = ctx.enter_context(nc.psum_tensor("ps_x", [128, 512], F32))

        s_small = sem("small_loaded")
        s_const = sem("constants_set")
        s_unit = sem("identity_copied")
        s_pre = [sem(f"statistics_x_loaded{i}") for i in range(P_RING)]
        s_read = sem("statistics_x_read")
        s_link = sem("dve_step")
        s_mean = sem("channel_means_made")
        s_var = sem("channel_variances_made")
        s_veps = sem("group_variance_plus_eps_made")
        s_ob = sem("value_bias_projected")
        s_ob2 = sem("output_bias_made")
        s_avg = sem("group_average_made")
        s_rt = sem("square_root_made")
        s_norm = sem("norm_tables_made")
        s_normb = sem("norm_of_sample_ready")
        s_xk = [sem(f"x_to_prepare_loaded{i}") for i in range(2)]
        s_g = sem("g_made")
        s_kq = sem("k_and_q_projected")
        s_kqc = sem("k_and_q_copied")
        s_hi_p = sem("hi_parts_made")
        s_lo_p = sem("lo_parts_made")
        s_vp = sem("v_projected")
        s_v = sem("v_copied")
        s_wr = [sem(f"parts_written{i}") for i in range(2)]
        s_ks = [sem(f"keys_stacked{i}") for i in range(2)]
        s_xt = [sem(f"x_to_add_loaded{i}") for i in range(2)]
        s_qs = [sem(f"query_stacked{i}") for i in range(4)]
        s_ms = [sem(f"row_scores_made{i}") for i in range(2)]
        s_mr = [sem(f"row_max_made{i}") for i in range(2)]
        s_neg = sem("negative_max_made")
        s_mhi = sem("max_hi_made")
        s_mp = sem("max_parts_made")
        s_mt = sem("max_transposed")
        s_mc = sem("max_rows_copied")
        s_mk = [sem(f"max_stacked{i}") for i in range(2)]
        s_t = sem("scores_made")
        s_e = sem("exp_made")
        s_pv = sem("values_product_made")
        s_add = sem("key_tiles_added")
        s_d = sem("row_sums_made")
        s_rc = sem("row_sums_inverted")
        s_n = sem("attention_divided")
        s_op = sem("output_projected")
        s_y = sem("y_made")
        s_st = sem("y_stats_made")
        s_ys = [sem(f"y_stored{i}") for i in range(2)]
        s_w = [sem(f"sweep_w_loaded{i}") for i in range(2)]
        s_whi = sem("sweep_w_hi_made")
        s_wsp = sem("sweep_w_split")
        s_yl = [sem(f"first_pair_y_loaded{i}") for i in range(2)]
        s_yl2 = sem("second_pair_y_loaded")
        s_xa = [sem(f"upper_rows_normalised{i}") for i in range(2)]
        s_xb = sem("lower_rows_normalised")
        s_xn = sem("second_pair_normalised")
        s_cv = [sem(f"conv_made{i}") for i in range(2)]
        s_new = [sem(f"new_row_made{i}") for i in range(2)]
        s_hi = [sem(f"row_hi_made{i}") for i in range(2)]
        s_lo = [sem(f"row_lo_made{i}") for i in range(2)]
        s_yb = [sem(f"y_reloaded{i}") for i in range(2)]
        s_yp = sem("pair_b_y_reloaded")
        s_fa = sem("first_pair_added")
        s_fb = sem("second_pair_added")
        s_out = sem("out_stored")

        HALF = T // 2
        FIRST_TILES = -(-T // TILE)
        TILES = IMAGES // TILE
        HALF_SIDE = SIDE // 2
        PG = PI // 4
        FINAL_SPLITS = 62
        FILL = 8 * (T - LEAD)

        def fill_tiles(b, s):
            if not filling(b) or s < FILL:
                return range(0)
            at = FIRST_TILES + 2 * (s - FILL) // 8
            return range(at, at + 1) if (s - FILL) % 4 == 0 and at < TILES else range(0)

        def filling(b):
            return isinstance(b, int) and b == -1

        def before_first(b, j):
            return isinstance(b, int) and b == 0 and j < LEAD

        def kq_bank(b, j):
            return ps_t[2] if before_first(b, j) and j % 2 else ps_x

        def v_bank(b, j):
            return ps_t[j % 2] if before_first(b, j) else ps_x

        def filled(b, s):
            return filling(b) and s == 8 * T - 1

        block = ctx.enter_context(nc.Block())

        FIRST, REST, ALL = slice(0, T), slice(T, IMAGES), slice(0, IMAGES)

        def scores_until(p):
            return UNIT0[p % T + 1] + p // T * ALL_UNITS

        def store(queue, pair, k, added):
            queue.wait_ge(added, k + 1)
            queue.dma_start(out_all[:, pair * PI + 4 * k:pair * PI + 4 * k + 4, :],
                            xs[pair][:, 4 * k:4 * k + 4, :, :].rearrange("c i h w -> c i (h w)")
                            ).then_inc(s_out, 16)

        def normalised(engine, rows, image):
            return engine.tensor_scalar(rows, rows, norm[:, 0, image:image + 1], norm[:, 1, image:image + 1],
                                        ALU.mult, ALU.add)

        def parts_of(row, c):
            return row[:, c, :].rearrange("c (p i) -> c p i", i=T)

        def place(d, j):
            return j if d % 2 == 0 else j * -1 + STEPS

        def line(xp, c, d, at):
            one = xp[:, c * T:c * T + T, bass.ds(at, 1), :] if d < 2 else xp[:, c * T:c * T + T, :, bass.ds(at, 1)]
            return one.rearrange("c i a w -> c (a w) i") if d < 2 else one.rearrange("c i h a -> c (h a) i")

        @block.sync
        def _(sp):
            sp.dma_start(cst[:, :], small).then_inc(s_small, 16)

            def load_tile(n):
                if n >= P_RING:
                    sp.wait_ge(s_read, n - P_RING + 1)
                sp.dma_start(probs[:, n % P_RING, :].rearrange("c (i l) -> c i l", l=L),
                             x_all[:, TILE * n:TILE * n + TILE, :]).then_inc(s_pre[n % P_RING], 16)

            for n in range(FIRST_TILES):
                load_tile(n)

            def load_x(b, j):
                sp.dma_start(x_k[:, j % 2, :], x_b[b][PREP[j], :, :]).then_inc(s_xk[j % 2], 16)

            load_x(0, 0)
            load_x(0, 1)

            def body(b, slots):
                for s in slots:
                    i, r = divmod(s, 8)
                    for n in fill_tiles(b, s):
                        load_tile(n)
                    if r == 3 and filling(b) and prepared(b, i):
                        bp, j = prepared(b, i)
                        sp.wait_ge(s_g, j + 1)
                        load_x(bp, j + 2)
                    if r == 0:
                        nxt = prepared(b, i + 1) if i + 1 < T else prepared(b + 1, 0)
                        if nxt and not (isinstance(nxt[0], int) and nxt[0] == 0 and nxt[1] < LEAD + 2):
                            load_x(*nxt)
                        if live(b, i - 1):
                            db, p = divmod(i - 1, T)
                            if not prepared(b, i - 1):
                                need(sp, s_y, b + db, T, p - 1)
                            sp.dma_start(x_t[:, p % 2, :], x_b[b + db][ORDER[p], :, :]).then_inc(s_xt[p % 2], 16)
                    if r == 7 and prepared(b, i):
                        bp, j = prepared(b, i)
                        need(sp, s_lo_p, bp, T, j + 1)
                        sp.dma_start(parts_dram[PREP[j]].rearrange("k c l -> c k l"),
                                     parts[:, :, :].bitcast(F32)).then_inc(s_wr[j % 2], 16)
                    before = prepared(b, i - 1)
                    if r == 7 and before:
                        bp, j = before
                        m = PREP[j]
                        need(sp, s_wr[j % 2], bp, 16 * HALF, 16 * (j // 2 + 1))
                        if not prepared(b, i):
                            need(sp, s_ks[j % 2], bp, 48 * HALF, 48 * (j // 2))
                        for row, part in enumerate((0, 1, 0)):
                            sp.dma_start(kstack[DH * row:DH * row + DH, m, :, :].bitcast(F32),
                                         parts_dram[m, part].rearrange("(h d) l -> d h l", d=DH)
                                         ).then_inc(s_ks[j % 2], 16)
                    if r == 5 and live(b, i + 3):
                        db, p = divmod(i + 3, T)
                        need(sp, s_t, b + db, 2 * ALL_UNITS, 2 * scores_until(place_before(p)))
                        for row, part in enumerate((2, 2, 3)):
                            sp.dma_start(qstack[DH * row:DH * row + DH, PLACE[p], :, :].bitcast(F32),
                                         parts_dram[ORDER[p], part].rearrange("(h d) l -> d h l", d=DH)
                                         ).then_inc(s_qs[PLACE[p]], 16)

            walk(sp, body)

            for i in range(2):
                sp.wait_ge(s_ys[i], 16 * 2 * HALF)
            sp.wait_ge(s_t, 2 * ALL_UNITS * B)
            for c in range(2):
                sp.dma_start(xs[0][:, c * T:c * T + T, :, :].rearrange("c i h w -> c i (h w)"),
                             y_all[:, c * T:c * T + T, :]).then_inc(s_yl[c], 16)
            sp.wait_ge(s_st, IMAGES)
            for d in range(2):
                sp.dma_start(w_raw[:, d, :], w_sweep[:, d, :]).then_inc(s_w[d], 16)
            for i in range(2):
                sp.wait_ge(s_ys[i], 16 * B * HALF)
            for d in range(2, 4):
                sp.wait_ge(s_wsp, d - 1)
                sp.dma_start(w_raw[:, d - 2, :], w_sweep[:, d, :]).then_inc(s_w[d - 2], 16)
            for k in range(PG):
                sp.dma_start(xs[1][:, 4 * k:4 * k + 4, :, :].rearrange("c i h w -> c i (h w)"),
                             y_all[:, PI + 4 * k:PI + 4 * k + 4, :]).then_inc(s_yl2, 16)
            for k in range(PG):
                if k >= 2:
                    sp.wait_ge(s_fa, k - 1)
                sp.dma_start(y_back[:, k % 2, :].rearrange("c (i l) -> c i l", l=L),
                             y_all[:, 4 * k:4 * k + 4, :]).then_inc(s_yb[k % 2], 16)
                if k >= 1:
                    store(sp, 0, k - 1, s_fa)
            store(sp, 0, PG - 1, s_fa)
            sp.wait_ge(s_out, 16 * PG)
            sp.dma_start(xs[0][:, :, :, :].rearrange("c i h w -> c i (h w)"),
                         y_all[:, PI:2 * PI, :]).then_inc(s_yp, 16)
            for k in range(PG):
                store(sp, 1, k, s_fb)
            sp.wait_ge(s_out, 16 * 2 * PG)

        @block.gpsimd
        def _(pool):
            pool.memset(ones[:, :], 1.0).then_inc(s_const, 1)
            pool.wait_ge(s_const, 1)
            pool.memset(kstack[PARTS:ROWS, :, :, :].bitcast(F32), 1.0).then_inc(s_const, 1)

            def body(b, slots):
                for s in slots:
                    i, r = divmod(s, 8)
                    if r == 7 and prepared(b, i):
                        bp, j = prepared(b, i)
                        need(pool, s_hi_p, bp, T, j + 1)
                        both = parts[:, :, :].rearrange("c (a k) l -> c a k l", k=2)
                        nc.gpsimd.tensor_tensor(both[:, :, 1, :], kq[:, :, :], both[:, :, 0, :].bitcast(F32),
                                                ALU.subtract).then_inc(s_lo_p, 1)
                    q, u = divmod(s - 2, 8)
                    if live(b, q):
                        db, p = divmod(q, T)
                        if u in (0, 4, 6) and u < 2 * len(KEYS[p]):
                            k = (0, 0, 1, 2)[u // 2]
                            tile, place = UNIT0[p] + u, (SUM0[p] + k) % S_RING
                            need(pool, s_e, b + db, 2 * ALL_UNITS, 2 * tile + 4)
                            need(pool, s_d, b + db, ALL_SUMS, SUM0[p] + k - S_RING + 1)
                            nc.gpsimd.tensor_tensor(sums[:, place, :], probs[:, tile % P_RING, :],
                                                    probs[:, (tile + 1) % P_RING, :], ALU.add).then_inc(s_add, 1)
                        elif u in (1, 2):
                            tile, place = UNIT0[p] + u + 1, SUM0[p] % S_RING
                            need(pool, s_e, b + db, 2 * ALL_UNITS, 2 * tile + 2)
                            need(pool, s_add, b + db, ALL_ADDS, ADD0[p] + u)
                            nc.gpsimd.tensor_tensor(sums[:, place, :], sums[:, place, :],
                                                    probs[:, tile % P_RING, :], ALU.add).then_inc(s_add, 1)

            walk(pool, body)
            pool.wait_ge(s_norm, 3)
            for c in range(2):
                pool.wait_ge(s_yl[c], 16)
                for i in range(c * T, c * T + T):
                    last = normalised(nc.gpsimd, xs[0][:, i, HALF_SIDE:SIDE, :], i)
            last.then_inc(s_xb, 1)
            pool.wait_ge(s_yl2, 16 * PG)
            for i in range(PI):
                last = normalised(nc.gpsimd, xs[1][:, i, :, :], PI + i)
            last.then_inc(s_xn, 1)
            for c in range(2):
                pool.wait_ge(s_lo[c], FINAL_SPLITS)
            for k in range(PG):
                pool.wait_ge(s_yb[k % 2], 16 * (k // 2 + 1))
                part = xs[0][:, 4 * k:4 * k + 4, :, :].rearrange("c i h w -> c (i h w)")
                nc.gpsimd.tensor_tensor(part, part, y_back[:, k % 2, :], ALU.add).then_inc(s_fa, 1)

        @block.scalar
        def _(act):
            def square_root(which, images):
                act.wait_ge(s_veps, which + 1)
                nc.scalar.activation(work[:, 3, images], work[:, 2, images], ACT.Sqrt).then_inc(s_rt, 1)

            square_root(0, FIRST)

            def body(b, slots):
                for s in slots:
                    i, r = divmod(s, 8)
                    if r == 0 and prepared(b, i - 1):
                        bp, j = prepared(b, i - 1)
                        need(act, s_vp, bp, T, j + 1)
                        need(act, s_pv, bp - 1, ALL_UNITS, UNIT0[LAST_USE[PREP[j]] + 1])
                        nc.scalar.activation(v[:, PREP[j], :], v_bank(bp, j)[:, 0:QT * C], ACT.Copy).then_inc(s_v, 1)
                    if r == 5 and live(b, i + 1):
                        db, p = divmod(i + 1, T)
                        need(act, s_mc, b + db, T, p + 1)
                        for part in range(2):
                            act.dma_start(
                                qstack[PARTS + part:PARTS + part + 1, PLACE[p], :, :].bitcast(F32)
                                .rearrange("p h (k l) -> p (h k) l", l=128),
                                max_rows[UNITS * part:UNITS * part + UNITS, p % 2, :].bitcast(F32)
                            ).then_inc(s_mk[p % 2], 16)
                    if r == 4 and live(b, i + 1):
                        db, p = divmod(i + 1, T)
                        need(act, s_mt, b + db, T, p + 1)
                        need(act, s_mk[p % 2], b + db, 32 * HALF, 32 * (p // 2))
                        nc.scalar.activation(max_rows[:, p % 2, :], ps_x[0:2 * UNITS, 0:128], ACT.Copy).then_inc(s_mc, 1)
                    if live(b, i) and i < T and r < 2 * len(KEYS[i]):
                        n = UNIT0[i] + r
                        for half in range(2):
                            need(act, s_t, b, 2 * ALL_UNITS, 2 * n + half + 1)
                            if half == 0:
                                need(act, s_pv, b, ALL_UNITS, n - P_RING + 1)
                                need(act, s_add, b, ALL_ADDS, tiles_added(n - P_RING))
                            nc.scalar.activation(probs[:, n % P_RING, 512 * half:512 * half + 512],
                                                 ps_t[(2 * n + half) % 3][:, :], ACT.Exp,
                                                 scale=SCALE).then_inc(s_e, 1)
                    if r == 0 and prepared(b, i):
                        bp, j = prepared(b, i)
                        m = PREP[j]
                        if j == 0:
                            need(act, s_normb, bp, 1, 1)
                        need(act, s_xk[j % 2], bp, 16 * HALF, 16 * (j // 2 + 1))
                        need(act, s_vp, bp, T, j - 1)
                        nc.scalar.activation(g[:, j % 2, :], x_k[:, j % 2, :], ACT.Identity,
                                             scale=norm_b[:, 0, m:m + 1], bias=norm_b[:, 1, m:m + 1]).then_inc(s_g, 1)
                    if r == 5 and prepared(b, i):
                        bp, j = prepared(b, i)
                        need(act, s_kq, bp, T, j + 1)
                        need(act, s_lo_p, bp, T, j)
                        for k, bias in enumerate((B_K, B_Q)):
                            nc.scalar.activation(kq[:, k, :], kq_bank(bp, j)[:, L * k:L * k + L], ACT.Identity,
                                                 bias=cst[:, bias:bias + 1]).then_inc(s_kqc, 1)
                    if r == 6 and prepared(b, i):
                        bp, j = prepared(b, i)
                        need(act, s_wr[(j - 1) % 2], bp, 16 * HALF, 16 * ((j + 1) // 2))
                        need(act, s_kqc, bp, 2 * T, 2 * j + 2)
                        both = parts[:, :, :].rearrange("c (a k) l -> c a k l", k=2)
                        nc.scalar.activation(both[:, :, 0, :], kq[:, :, :], ACT.Copy).then_inc(s_hi_p, 1)
                    if r == 2 and live(b, i - 2):
                        db, p = divmod(i - 2, T)
                        need(act, s_y, b + db, T, p + 1)
                        act.dma_start(y_b[b + db][ORDER[p], :, :], y_t[:, p % 2, :]).then_inc(s_ys[p % 2], 16)
                    if filled(b, s):
                        square_root(1, REST)

            walk(act, body)
            square_root(2, ALL)

            act.wait_ge(s_norm, 3)
            act.wait_ge(s_yl[1], 16)
            for i in range(T, 2 * T):
                rows = xs[0][:, i, 0:HALF_SIDE, :]
                last = nc.scalar.activation(rows, rows, ACT.Identity, scale=norm[:, 0, i:i + 1],
                                            bias=norm[:, 1, i:i + 1])
            last.then_inc(s_xa[1], 1)
            for pair in range(2):
                done, splits = 4 * STEPS * pair, FINAL_SPLITS * pair
                for d in range(4):
                    if d % 2 == 0:
                        if d == 0 and pair == 1:
                            act.wait_ge(s_xn, 1)
                        for c in range(2):
                            if d == 0 and pair == 0:
                                act.wait_ge(s_xa[c], 1)
                            if splits:
                                act.wait_ge(s_lo[c], splits)
                            nc.scalar.activation(parts_of(row_hi, c), line(xs[pair], c, d, 0),
                                                 ACT.Copy).then_inc(s_hi[c], 1)
                        splits += 1
                    with act.Fori(1, STEPS + 1) as j:
                        for c in range(2):
                            act.wait_ge(s_new[c], j + done)
                            nc.scalar.activation(parts_of(row_hi, c), line(xs[pair], c, d, place(d, j)),
                                                 ACT.Copy).then_inc(s_hi[c], 1)
                    done += STEPS
                    splits += STEPS

        @block.vector
        def _(dve):
            vec = nc.vector
            links = [0]

            def link(ins):
                links[0] += 1
                ins.then_inc(s_link, 1)
                dve.wait_ge(s_link, links[0])

            def norm_tables(which, images):
                mean, var, t2, root, scratch = (work[:, i, images] for i in range(5))
                stat = [stats[:, images, k] for k in range(6)]
                scale, bias = norm[:, 0, images], norm[:, 1, images]
                link(vec.tensor_tensor(t2, stat[1], stat[4], ALU.subtract))
                link(vec.tensor_scalar(scratch, t2, 0.5, None, ALU.mult))
                link(vec.tensor_tensor(t2, scratch, scratch, ALU.mult))
                link(vec.tensor_tensor(var, stat[2], stat[5], ALU.add))
                link(vec.scalar_tensor_tensor(var, var, 1.0 / L, t2, ALU.mult, ALU.add))
                link(vec.tensor_tensor(scratch, stat[1], stat[4], ALU.add))
                vec.tensor_scalar(mean, scratch, 0.5, None, ALU.mult).then_inc(s_mean, 1)
                dve.wait_ge(s_avg, 2 * which + 1)
                link(vec.tensor_tensor(t2, mean, ps_x[:, images], ALU.subtract))
                link(vec.tensor_tensor(scratch, t2, t2, ALU.mult))
                link(vec.tensor_scalar(bias, ps_x[:, images], -1.0, None, ALU.mult))
                vec.tensor_tensor(var, scratch, var, ALU.add).then_inc(s_var, 1)
                dve.wait_ge(s_avg, 2 * which + 2)
                vec.tensor_scalar(t2, ps_x[:, slice(images.start + 128, images.stop + 128)], 1e-5, None,
                                  ALU.add).then_inc(s_veps, 1)
                dve.wait_ge(s_rt, which + 1)
                link(vec.reciprocal(scale, root))
                link(vec.tensor_tensor(scratch, scale, scale, ALU.mult))
                link(vec.tensor_tensor(scratch, scratch, t2, ALU.mult))
                link(vec.tensor_scalar(scratch, scratch, -0.5, 1.5, ALU.mult, ALU.add))
                link(vec.tensor_tensor(scale, scale, scratch, ALU.mult))
                vec.tensor_tensor(bias, bias, scale, ALU.mult).then_inc(s_norm, 1)
                dve.wait_ge(s_norm, which + 1)

            def read_tile(n):
                dve.wait_ge(s_pre[n % P_RING], 16 * (n // P_RING + 1))
                for k in range(TILE):
                    last = vec.bn_stats(stats[:, TILE * n + k, :], probs[:, n % P_RING, L * k:L * k + L])
                last.then_inc(s_read, 1)

            for n in range(FIRST_TILES):
                read_tile(n)
            dve.wait_ge(s_read, FIRST_TILES)
            dve.wait_ge(s_small, 16)
            dve.wait_ge(s_ob, 1)
            vec.tensor_scalar(out_bias[:, :], ps_x[:, 256:257], cst[:, B_O:B_O + 1], None, ALU.add).then_inc(s_ob2, 1)
            vec.tensor_copy(unit[:, :], cst[:, IDENT:IDENT + 128]).then_inc(s_unit, 1)
            norm_tables(0, FIRST)

            def body(b, slots):
                def row_maxima(p, db, w, half):
                    n = len(KEYS[p][2 * half:2 * half + 2])
                    need(dve, s_ms[half], b + db, T * UNITS, UNITS * p + w + 1)
                    vec.tensor_reduce(row_max[:, p % 2, w, half:half + 1], ps_m[half][:, 0:n * L],
                                      AX.X, ALU.max).then_inc(s_mr[half], 1)

                def invert(p, db, piece):
                    part = slice(L // 4 * piece, L // 4 * piece + L // 4)
                    if piece == 0:
                        need(dve, s_d, b + db, ALL_SUMS, SUM0[p + 1])
                        need(dve, s_n, b + db, T, p)
                    vec.reciprocal(recip[:, part], ps_o[p % 2][:, L + part.start:L + part.stop]).then_inc(s_rc, 1)

                for s in slots:
                    i, r = divmod(s, 8)
                    prep = prepared(b, i)
                    for n in fill_tiles(b, s - 12):
                        read_tile(n)
                    if r == 2 and live(b, i + 1):
                        db, p = divmod(i + 1, T)
                        need(dve, s_mt, b + db, T, p - 1)
                        need(dve, s_neg, b + db, T, p + 1)
                        vec.tensor_copy(max_parts[:, p % 2, 0:UNITS], neg_max[:, :]).then_inc(s_mhi, 1)
                    q, w = divmod(s + 14, 8)
                    if live(b, q):
                        db, p = divmod(q, T)
                        row_maxima(p, db, w, 0)
                    if r == 2 and live(b, i + 1):
                        db, p = divmod(i + 1, T)
                        need(dve, s_mhi, b + db, T, p + 1)
                        vec.tensor_tensor(max_parts[:, p % 2, UNITS:2 * UNITS], neg_max[:, :],
                                          max_parts[:, p % 2, 0:UNITS].bitcast(F32),
                                          ALU.subtract).then_inc(s_mp, 1)
                    if live(b, q):
                        db, p = divmod(q, T)
                        row_maxima(p, db, w, 1)
                    if r == 1 and live(b, i - 2):
                        db, p = divmod(i - 2, T)
                        need(dve, s_op, b + db, T, p + 1)
                        need(dve, s_xt[p % 2], b + db, 16 * HALF, 16 * (p // 2 + 1))
                        need(dve, s_ys[p % 2], b + db, 16 * HALF, 16 * (p // 2))
                        vec.scalar_tensor_tensor(y_t[:, p % 2, :], ps_x[:, 0:L], out_bias[:, 0:1],
                                                 x_t[:, p % 2, :], ALU.add, ALU.add).then_inc(s_y, 1)
                    if r == 1 and live(b, i + 1):
                        db, p = divmod(i + 1, T)
                        for half in range(2):
                            need(dve, s_mr[half], b + db, T * UNITS, UNITS * (p + 1))
                        vec.tensor_reduce(neg_max[:, :], row_max[:, p % 2, :, :], AX.X, ALU.max,
                                          negate=True).then_inc(s_neg, 1)
                    if r == 0 and prep and prep[1] == 0:
                        bp, j = prep
                        need(dve, s_g, bp, T, 0)
                        vec.tensor_copy(norm_b[:, :, :], norm[:, :, bass.ds(bp * T, T)]).then_inc(s_normb, 1)
                    if r == 0 and live(b, i - 3):
                        db, p = divmod(i - 3, T)
                        need(dve, s_y, b + db, T, p + 1)
                        vec.bn_stats(stats[:, bass.ds((b + db) * T + ORDER[p], 1), :].rearrange("c a k -> c (a k)"),
                                     y_t[:, p % 2, :]).then_inc(s_st, 1)
                    if 3 <= r < 7 and live(b, i - 1):
                        db, p = divmod(i - 1, T)
                        invert(p, db, r - 3)
                    if r == 7 and live(b, i - 1):
                        db, p = divmod(i - 1, T)
                        need(dve, s_rc, b + db, 4 * T, 4 * p + 4)
                        need(dve, s_op, b + db, T, p - 1)
                        vec.tensor_tensor(attn[:, p % 2, :], ps_o[p % 2][:, 0:L], recip[:, :],
                                          ALU.mult).then_inc(s_n, 1)
                    if filled(b, s):
                        dve.wait_ge(s_read, TILES)
                        norm_tables(1, REST)

            walk(dve, body)

            dve.wait_ge(s_st, IMAGES)
            norm_tables(2, ALL)
            def split_weights(d):
                dve.wait_ge(s_w[d % 2], 16 * (d // 2 + 1))
                vec.tensor_copy(w_hi[:, d, :], w_raw[:, d % 2, :]).then_inc(s_whi, 1)
                dve.wait_ge(s_whi, d + 1)
                vec.tensor_tensor(w_lo[:, d, :], w_raw[:, d % 2, :], w_hi[:, d, :].bitcast(F32),
                                  ALU.subtract).then_inc(s_wsp, 1)

            dve.wait_ge(s_yl[0], 16)
            for i in range(T):
                last = normalised(vec, xs[0][:, i, 0:HALF_SIDE, :], i)
            last.then_inc(s_xa[0], 1)
            for i in range(2):
                dve.wait_ge(s_ys[i], 16 * B * HALF)
            split_weights(0)
            for pair in range(2):
                done, splits = 4 * STEPS * pair, FINAL_SPLITS * pair

                def row_parts(c, d, at, count):
                    dve.wait_ge(s_hi[c], count)
                    vec.tensor_tensor(parts_of(row_lo, c), line(xs[pair], c, d, at),
                                      parts_of(row_hi, c).bitcast(F32), ALU.subtract).then_inc(s_lo[c], 1)

                for d in range(4):
                    if d % 2 == 0:
                        splits += 1
                        for c in range(2):
                            row_parts(c, d, 0, splits)
                    first = pair == 0 and d == 0
                    for start, end in ((1, HALF_SIDE), (HALF_SIDE, STEPS + 1)) if first else ((1, STEPS + 1),):
                        if start == HALF_SIDE:
                            split_weights(1)
                            dve.wait_ge(s_xb, 1)
                        with dve.Fori(start, end) as j:
                            at = dve.snap(place(d, j))
                            for c in range(2):
                                dve.wait_ge(s_cv[c], j + done)
                                now = line(xs[pair], c, d, at)
                                vec.scalar_tensor_tensor(now, ps_t[c][:, 0:SIDE * T].rearrange("c (p i) -> c p i", i=T),
                                                         0.0, now, ALU.max, ALU.add).then_inc(s_new[c], 1)
                                row_parts(c, d, at, j + splits)
                    if pair == 0 and d == 0:
                        split_weights(2)
                        split_weights(3)
                    done += STEPS
                    splits += STEPS
            for c in range(2):
                dve.wait_ge(s_lo[c], 2 * FINAL_SPLITS)
            dve.wait_ge(s_yp, 16)
            for k in range(PG):
                part = xs[1][:, 4 * k:4 * k + 4, :, :].rearrange("c i h w -> c (i h w)")
                back = xs[0][:, 4 * k:4 * k + 4, :, :].rearrange("c i h w -> c (i h w)")
                vec.tensor_tensor(part, part, back, ALU.add).then_inc(s_fb, 1)

        @block.tensor
        def _(pe):
            mm = nc.tensor.matmul

            def group_averages(which, images):
                pe.wait_ge(s_mean, which + 1)
                mm(ps_x[:, images], cst[:, AVG:AVG + 128], work[:, 0, images], start=True, stop=True).then_inc(s_avg, 1)
                pe.wait_ge(s_var, which + 1)
                mm(ps_x[:, slice(images.start + 128, images.stop + 128)], cst[:, AVG:AVG + 128],
                   work[:, 1, images], start=True, stop=True).then_inc(s_avg, 1)

            pe.wait_ge(s_small, 16)
            mm(ps_x[:, 256:257], cst[:, W_O:W_O + 128], cst[:, B_V:B_V + 1], start=True, stop=True).then_inc(s_ob, 1)
            pe.wait_ge(s_ob2, 1)
            group_averages(0, FIRST)
            pe.wait_ge(s_unit, 1)
            pe.wait_ge(s_const, 2)

            def row_scores(b, p, w, half):
                h, qt = divmod(w, QT)
                need(pe, s_mr[half], b, T * UNITS, UNITS * p + w)
                for k, m in enumerate(KEYS[p][2 * half:2 * half + 2]):
                    last = mm(ps_m[half][:, L * k:L * k + L], qstack[0:PARTS, PLACE[p], h, 128 * qt:128 * qt + 128],
                              kstack[0:PARTS, m, h, :], start=True, stop=True)
                last.then_inc(s_ms[half], 1)

            def body(b, slots):
                for s in slots:
                    i, r = divmod(s, 8)
                    prep = prepared(b, i)
                    q, w = divmod(s + 14, 8)
                    if live(b, q):
                        db, p = divmod(q, T)
                        if w == 0:
                            for k in range(2):
                                need(pe, s_ks[k], b + db, 48 * HALF, 48 * ((NEEDS[p] - k) // 2 + 1))
                            need(pe, s_qs[PLACE[p]], b + db, 48 * PLACE_USES[PLACE[p]],
                                 48 * PLACE[:p + 1].count(PLACE[p]))
                        row_scores(b + db, p, w, 0)
                    if live(b, i) and i < T and r < 2 * len(KEYS[i]):
                        n = UNIT0[i] + r
                        m, kt = KEYS[i][r // 2], r % 2
                        if isinstance(b, int) and b == 0 and n == 0:
                            pe.wait_ge(s_v, LEAD)
                        if r == 0:
                            need(pe, s_mk[i % 2], b, 32 * HALF, 32 * (i // 2 + 1))
                        for half in range(2):
                            need(pe, s_e, b, 2 * ALL_UNITS, 2 * n + half - 2)
                            for k in range(2):
                                last = mm(ps_t[(2 * n + half) % 3][:, L * k:L * k + L],
                                          kstack[0:ROWS, m, 2 * half + k, 128 * kt:128 * kt + 128],
                                          qstack[0:ROWS, PLACE[i], 2 * half + k, :], start=True, stop=True)
                            last.then_inc(s_t, 1)
                    q, w = divmod(s + 14, 8)
                    if live(b, q):
                        db, p = divmod(q, T)
                        row_scores(b + db, p, w, 1)
                    q, u = divmod(s - 1, 8)
                    if live(b, q) and q < T and u < 2 * len(KEYS[q % T]):
                        db, p = divmod(q, T)
                        n = UNIT0[p] + u
                        m, kt = KEYS[p][u // 2], u % 2
                        if u == 0:
                            need(pe, s_n, b + db, T, p - 1)
                            need(pe, s_v, b + db, T, NEEDS[p] + 1)
                        need(pe, s_e, b + db, 2 * ALL_UNITS, 2 * n + 2)
                        for h in range(HEADS):
                            last = mm(ps_o[p % 2][DH * h:DH * h + DH, 0:L],
                                      v[:, m, C * kt + DH * h:C * kt + DH * h + DH],
                                      probs[:, n % P_RING, L * h:L * h + L],
                                      start=(u == 0), stop=(u == 2 * len(KEYS[p]) - 1), skip_group_check=True)
                        last.then_inc(s_pv, 1)
                    q, u = divmod(s - 6, 8)
                    if u % 2 == 0 and live(b, q) and u // 2 < len(KEYS[q % T]) - 1:
                        db, p = divmod(q, T)
                        n = SUM0[p] + u // 2
                        need(pe, s_add, b + db, ALL_ADDS, ADD0[p] + 3 + u // 2)
                        for h in range(HEADS):
                            last = mm(ps_o[p % 2][DH * h:DH * h + DH, L:2 * L], ones[:, :],
                                      sums[:, n % S_RING, L * h:L * h + L],
                                      start=False, stop=(u // 2 == len(KEYS[p]) - 2), skip_group_check=True)
                        last.then_inc(s_d, 1)
                    if r == 0 and live(b, i - 2):
                        db, p = divmod(i - 2, T)
                        bank_read(b, i)
                        need(pe, s_n, b + db, T, p + 1)
                        mm(ps_x[:, 0:L], cst[:, W_O:W_O + 128], attn[:, p % 2, :], start=True, stop=True).then_inc(s_op, 1)
                    if r == 3 and live(b, i + 1):
                        db, p = divmod(i + 1, T)
                        if live(b, i - 2):
                            need(pe, s_y, b, T, i - 1)
                        else:
                            bank_read(b, i)
                        need(pe, s_mp, b + db, T, p + 1)
                        mm(ps_x[0:2 * UNITS, 0:128], max_parts[:, p % 2, :], unit[:, :],
                           start=True, stop=True).then_inc(s_mt, 1)
                    if r == 4 and prep:
                        bp, j = prep
                        if filling(b):
                            need(pe, s_kqc, bp, 2 * T, 2 * j - 2)
                        elif live(b, i + 1):
                            db, p = divmod(i + 1, T)
                            need(pe, s_mc, b + db, T, p + 1)
                        else:
                            bank_read(b, i)
                        need(pe, s_ks[(j - 1) % 2], bp, 48 * HALF, 48 * ((j - 1) // 2))
                        need(pe, s_g, bp, T, j + 1)
                        bank = kq_bank(bp, j)
                        mm(bank[:, 0:L], cst[:, W_K:W_K + 128], g[:, j % 2, :], start=True, stop=True)
                        mm(bank[:, L:2 * L], cst[:, W_Q:W_Q + 128], g[:, j % 2, :],
                           start=True, stop=True).then_inc(s_kq, 1)
                    if r == 7 and prep:
                        bp, j = prep
                        if filling(b):
                            need(pe, s_v, bp, T, j - 1)
                        else:
                            need(pe, s_kqc, bp, 2 * T, 2 * j + 2)
                        bank = v_bank(bp, j)
                        for kt in range(QT):
                            last = mm(bank[:, C * kt:C * kt + C], g[:, j % 2, 128 * kt:128 * kt + 128],
                                      cst[:, W_V:W_V + 128], start=True, stop=True)
                        last.then_inc(s_vp, 1)
                    if filled(b, s):
                        pe.wait_ge(s_mc, 1)
                        group_averages(1, REST)

            def bank_read(b, i):
                if prepared(b, i - 1):
                    bp, j = prepared(b, i - 1)
                    need(pe, s_v, bp, T, j + 1)
                elif live(b, i):
                    need(pe, s_mc, b, T, i + 1)

            walk(pe, body)

            group_averages(2, ALL)
            for pair in range(2):
                done, splits = 0, FINAL_SPLITS * pair
                for d in range(4):
                    if pair == 0:
                        pe.wait_ge(s_wsp, d + 1)
                    if d % 2 == 0:
                        splits += 1
                    with pe.Fori(0, STEPS) as j:
                        for c in range(2):
                            pe.wait_ge(s_lo[c], j + splits)
                            taps = sorted(range(TAPS), key=lambda k: abs(k - TAPS // 2))
                            for k in taps:
                                shift = k - TAPS // 2
                                lo, hi = max(0, -shift) * T, (SIDE - max(0, shift)) * T
                                for w, row in ((w_hi, row_hi), (w_lo, row_hi), (w_hi, row_lo)):
                                    last = mm(ps_t[c][:, lo:hi], w[:, d, C * k:C * k + C],
                                              row[:, c, lo + shift * T:hi + shift * T],
                                              start=(k == taps[0] and w is w_hi and row is row_hi),
                                              stop=(k == taps[-1] and row is row_lo))
                            last.then_inc(s_cv[c], 1)
                    splits += STEPS


def kernel(x, L0_conv_w_in, L0_conv_b_in, L0_conv_w_out, L0_conv_b_out,
           L1_conv_w_down, L1_conv_w_up, L1_conv_w_right, L1_conv_w_left):
    import concourse.bacc as _bacc
    from concourse.bass_utils import run_bass_kernel_spmd as _run

    w_in = np.asarray(L0_conv_w_in)
    average = np.kron(np.eye(C // GROUP, dtype=np.float32), np.full((GROUP, GROUP), 1.0 / GROUP, np.float32))
    small = np.concatenate(
        [w_in[C * i:C * i + C].T for i in range(3)]
        + [np.asarray(L0_conv_w_out).T, average, np.eye(128, dtype=np.float32),
           np.asarray(L0_conv_b_in).reshape(3, C).T, np.asarray(L0_conv_b_out).reshape(C, 1)], axis=1)
    sweeps = np.stack([np.asarray(w) for w in (L1_conv_w_down, L1_conv_w_up, L1_conv_w_right, L1_conv_w_left)])
    arrays = {
        "x_dram": np.ascontiguousarray(np.asarray(x).reshape(IMAGES, C, L)),
        "small_dram": np.ascontiguousarray(small),
        "sweep_dram": np.ascontiguousarray(sweeps.transpose(2, 0, 3, 1).reshape(C, 4, TAPS * C)),
    }
    nc = _bacc.Bacc("TRN2", target_bir_lowering=False, num_devices=1)
    args = [nc.dram_tensor(name, a.shape, F32, kind="ExternalInput").ap() for name, a in arrays.items()]
    out = nc.dram_tensor("out_dram", (IMAGES, C, L), F32, kind="ExternalOutput").ap()
    build(nc, *args, out)
    r = _run(nc, [arrays], core_ids=[0])
    return r.results[0]["out_dram"].reshape(IMAGES, C, SIDE, SIDE)
```
